# Optimizing a Trainium2 kernel written in Bass

```python
import numpy as np
import jax
import jax.numpy as jnp

def _softmax(x, axis=-1):
    return jax.nn.softmax(x, axis=axis)

def _gelu(x):
    return jax.nn.gelu(x, approximate=True)

def _silu(x):
    return jax.nn.silu(x)

def _sigmoid(x):
    return jax.nn.sigmoid(x)

def _layernorm(x, axis=-1, eps=1e-05):
    m = jnp.mean(x, axis=axis, keepdims=True)
    v = jnp.var(x, axis=axis, keepdims=True)
    return (x - m) / jnp.sqrt(v + eps)

def _scatter_add(tgt, idx, src, axis=0):
    return tgt.at[idx].add(src)

def _segment_sum(src, seg, n):
    return jax.ops.segment_sum(src, seg, n)
kernel_name = 'mk_gnn_preln_d4_gnn_r16_076292'

def setup_inputs(seed: int=0):
    np.random.seed(seed)
    _w = jnp.asarray

    def _rec_inputs():
        import jax
        import jax.numpy as jnp
        _gk = jax.random.key(seed)
        x = -0.0002928 + 1 * jax.random.normal(jax.random.fold_in(_gk, 1), (512, 512), jnp.float32)
        src = jax.random.randint(jax.random.fold_in(_gk, 2), (16384,), 0, 512, jnp.int32)
        dst = jax.random.randint(jax.random.fold_in(_gk, 3), (16384,), 0, 512, jnp.int32)
        _o = jnp.argsort(dst, stable=True)
        src = src[_o]
        dst = dst[_o]
        edge_type_4 = jax.random.randint(jax.random.fold_in(_gk, 12), (16384,), 0, 4, jnp.int32)
        edge_weight = jax.random.uniform(jax.random.fold_in(_gk, 13), (16384,), jnp.float32, 0.0, 0.999995)
        return (x, src, dst, edge_type_4, edge_weight)
    x, src, dst, edge_type_4, edge_weight = _rec_inputs()

    def _L0_gnn_setup():
        import jax, jax.numpy as jnp
        import numpy as np
        N = 512
        D = 512
        E = 16384
        STEPS = 3
        key = jax.random.key(seed)
        k1, k2, k3 = jax.random.split(key, 3)
        x = jax.random.normal(k1, (N, D), dtype=jnp.float32)
        edge_index = jax.random.randint(k2, (2, E), 0, N, dtype=jnp.int32)
        W = jax.random.normal(k3, (D, D), dtype=jnp.float32) / np.sqrt(D)
        b = jnp.zeros((D,), dtype=jnp.float32)
        diffusion_weights = jnp.ones((STEPS + 1,), dtype=jnp.float32) / (STEPS + 1)
        return {'x': x, 'edge_index': edge_index, 'W': W, 'b': b, 'diffusion_weights': diffusion_weights}
    _L0_gnn_all = _L0_gnn_setup()
    _L0_gnn_in = {k: v for k, v in _L0_gnn_all.items() if k in ('W', 'b', 'diffusion_weights')}
    del _L0_gnn_all

    def _L1_gnn_setup():
        import jax, jax.numpy as jnp
        import numpy as np
        DIM = 512
        NUM_REL = 4
        N_NODES = 3125
        N_EDGES = 10000

        def _layer_norm(x, g, b, eps=1e-05):
            mu = jnp.mean(x, axis=-1, keepdims=True)
            var = jnp.mean((x - mu) ** 2, axis=-1, keepdims=True)
            return (x - mu) * jax.lax.rsqrt(var + eps) * g + b
        key = jax.random.key(seed)
        ks = jax.random.split(key, 16)
        s = 1.0 / np.sqrt(DIM)
        inp = {'x': jax.random.normal(ks[0], (N_NODES, DIM), jnp.float32), 'edge_index': jax.random.randint(ks[1], (2, N_EDGES), 0, N_NODES, jnp.int32), 'edge_type': jax.random.randint(ks[2], (N_EDGES,), 0, NUM_REL, jnp.int32), 'edge_weight': jax.random.uniform(ks[3], (N_EDGES,), jnp.float32), 'W_self': jax.random.uniform(ks[4], (DIM, DIM), jnp.float32, -s, s), 'b_self': jnp.zeros((DIM,), jnp.float32), 'W_rel': jax.random.uniform(ks[5], (NUM_REL, DIM, DIM), jnp.float32, -s, s), 'b_rel': jnp.zeros((NUM_REL, DIM), jnp.float32), 'ln1_g': jnp.ones((DIM,), jnp.float32), 'ln1_b': jnp.zeros((DIM,), jnp.float32), 'ln2_g': jnp.ones((DIM,), jnp.float32), 'ln2_b': jnp.zeros((DIM,), jnp.float32), 'W_ffn1': jax.random.uniform(ks[6], (DIM, 2 * DIM), jnp.float32, -s, s), 'b_ffn1': jnp.zeros((2 * DIM,), jnp.float32), 'W_ffn2': jax.random.uniform(ks[7], (2 * DIM, DIM), jnp.float32, -1.0 / np.sqrt(2 * DIM), 1.0 / np.sqrt(2 * DIM)), 'b_ffn2': jnp.zeros((DIM,), jnp.float32)}
        return inp
    _L1_gnn_all = _L1_gnn_setup()
    _L1_gnn_in = {k: v for k, v in _L1_gnn_all.items() if k in ('W_self', 'b_self', 'W_rel', 'b_rel', 'ln1_g', 'ln1_b', 'ln2_g', 'ln2_b', 'W_ffn1', 'b_ffn1', 'W_ffn2', 'b_ffn2')}
    del _L1_gnn_all

    def _L2_gnn_setup():
        import jax, jax.numpy as jnp
        import numpy as np
        N, E, D_IN, D_OUT = (512, 16384, 512, 512)
        key = jax.random.key(seed)
        k1, k2, k3 = jax.random.split(key, 3)
        x = jax.random.normal(k1, (N, D_IN), dtype=jnp.float32)
        edge_index = jax.random.randint(k2, (2, E), 0, N, dtype=jnp.int64)
        limit = float(np.sqrt(6.0 / (D_IN + D_OUT)))
        weight = jax.random.uniform(k3, (D_IN, D_OUT), dtype=jnp.float32, minval=-limit, maxval=limit)
        bias = jnp.zeros((D_OUT,), dtype=jnp.float32)
        return {'x': x, 'edge_index': edge_index, 'weight': weight, 'bias': bias}
    _L2_gnn_all = _L2_gnn_setup()
    _L2_gnn_in = {k: v for k, v in _L2_gnn_all.items() if k in ('weight', 'bias')}
    del _L2_gnn_all

    def _L3_gnn_setup():
        import jax, jax.numpy as jnp
        import numpy as np
        N_NODES = 625
        N_EDGES = 10000
        D = 512

        def _sage_conv(x, src, dst, Wl, bl, Wr, num_nodes):
            msg = x[src]
            agg = jax.ops.segment_sum(msg, dst, num_segments=num_nodes)
            cnt = jax.ops.segment_sum(jnp.ones((src.shape[0],), x.dtype), dst, num_segments=num_nodes)
            agg = agg / jnp.maximum(cnt, 1.0)[:, None]
            return agg @ Wl.T + bl + x @ Wr.T
        key = jax.random.key(seed)
        ks = jax.random.split(key, 8)
        s = 1.0 / np.sqrt(D)
        x = jax.random.normal(ks[0], (N_NODES, D), dtype=jnp.float32)
        edge_index = jax.random.randint(ks[1], (2, N_EDGES), 0, N_NODES, dtype=jnp.int64)
        Wl1 = jax.random.uniform(ks[2], (D, D), jnp.float32, -s, s)
        bl1 = jax.random.uniform(ks[3], (D,), jnp.float32, -s, s)
        Wr1 = jax.random.uniform(ks[4], (D, D), jnp.float32, -s, s)
        Wl2 = jax.random.uniform(ks[5], (D, D), jnp.float32, -s, s)
        bl2 = jax.random.uniform(ks[6], (D,), jnp.float32, -s, s)
        Wr2 = jax.random.uniform(ks[7], (D, D), jnp.float32, -s, s)
        return {'x': x, 'edge_index': edge_index, 'Wl1': Wl1, 'bl1': bl1, 'Wr1': Wr1, 'Wl2': Wl2, 'bl2': bl2, 'Wr2': Wr2}
    _L3_gnn_all = _L3_gnn_setup()
    _L3_gnn_in = {k: v for k, v in _L3_gnn_all.items() if k in ('Wl1', 'bl1', 'Wr1', 'Wl2', 'bl2', 'Wr2')}
    del _L3_gnn_all
    return {'x': x, 'src': src, 'dst': dst, 'edge_type_4': edge_type_4, 'edge_weight': edge_weight, 'L0_gnn_W': _L0_gnn_in['W'], 'L0_gnn_b': _L0_gnn_in['b'], 'L0_gnn_diffusion_weights': _L0_gnn_in['diffusion_weights'], 'L1_gnn_W_self': _L1_gnn_in['W_self'], 'L1_gnn_b_self': _L1_gnn_in['b_self'], 'L1_gnn_W_rel': _L1_gnn_in['W_rel'], 'L1_gnn_b_rel': _L1_gnn_in['b_rel'], 'L1_gnn_ln1_g': _L1_gnn_in['ln1_g'], 'L1_gnn_ln1_b': _L1_gnn_in['ln1_b'], 'L1_gnn_ln2_g': _L1_gnn_in['ln2_g'], 'L1_gnn_ln2_b': _L1_gnn_in['ln2_b'], 'L1_gnn_W_ffn1': _L1_gnn_in['W_ffn1'], 'L1_gnn_b_ffn1': _L1_gnn_in['b_ffn1'], 'L1_gnn_W_ffn2': _L1_gnn_in['W_ffn2'], 'L1_gnn_b_ffn2': _L1_gnn_in['b_ffn2'], 'L2_gnn_weight': _L2_gnn_in['weight'], 'L2_gnn_bias': _L2_gnn_in['bias'], 'L3_gnn_Wl1': _L3_gnn_in['Wl1'], 'L3_gnn_bl1': _L3_gnn_in['bl1'], 'L3_gnn_Wr1': _L3_gnn_in['Wr1'], 'L3_gnn_Wl2': _L3_gnn_in['Wl2'], 'L3_gnn_bl2': _L3_gnn_in['bl2'], 'L3_gnn_Wr2': _L3_gnn_in['Wr2']}

def reference(x, src, dst, edge_type_4, edge_weight, L0_gnn_W, L0_gnn_b, L0_gnn_diffusion_weights, L1_gnn_W_self, L1_gnn_b_self, L1_gnn_W_rel, L1_gnn_b_rel, L1_gnn_ln1_g, L1_gnn_ln1_b, L1_gnn_ln2_g, L1_gnn_ln2_b, L1_gnn_W_ffn1, L1_gnn_b_ffn1, L1_gnn_W_ffn2, L1_gnn_b_ffn2, L2_gnn_weight, L2_gnn_bias, L3_gnn_Wl1, L3_gnn_bl1, L3_gnn_Wr1, L3_gnn_Wl2, L3_gnn_bl2, L3_gnn_Wr2):
    import jax
    import jax.numpy as jnp

    def _L0_gnn_ref(x, edge_index, W, b, diffusion_weights):
        import jax, jax.numpy as jnp
        import numpy as np
        N = 512
        D = 512
        E = 16384
        STEPS = 3
        h = x @ W + b
        row, col = (edge_index[0], edge_index[1])
        adj = jnp.zeros((N, N), dtype=h.dtype)
        adj = adj.at[row, col].set(1.0)
        adj = adj.at[col, row].set(1.0)
        adj = adj + jnp.eye(N, dtype=h.dtype)
        row_sum = adj.sum(axis=1, keepdims=True)
        adj = adj / jnp.maximum(row_sum, 1.0)
        out = diffusion_weights[0] * h
        cur = h
        for i in range(STEPS):
            cur = adj @ cur
            out = out + diffusion_weights[i + 1] * cur
        return jax.nn.relu(out)

    def _L1_gnn_ref(x, edge_index, edge_type, edge_weight, W_self, b_self, W_rel, b_rel, ln1_g, ln1_b, ln2_g, ln2_b, W_ffn1, b_ffn1, W_ffn2, b_ffn2):
        import jax, jax.numpy as jnp
        import numpy as np
        DIM = 512
        NUM_REL = 4
        N_NODES = 3125
        N_EDGES = 10000

        def _layer_norm(x, g, b, eps=1e-05):
            mu = jnp.mean(x, axis=-1, keepdims=True)
            var = jnp.mean((x - mu) ** 2, axis=-1, keepdims=True)
            return (x - mu) * jax.lax.rsqrt(var + eps) * g + b
        n = x.shape[0]
        src, dst = (edge_index[0], edge_index[1])
        xs = x[src]
        total_msg = jnp.zeros_like(xs)
        for r in range(NUM_REL):
            w_r = jnp.where(edge_type == r, edge_weight, 0.0)
            total_msg = total_msg + (xs @ W_rel[r] + b_rel[r]) * w_r[:, None]
        agg = jax.ops.segment_sum(total_msg, dst, num_segments=n)
        deg = jax.ops.segment_sum(edge_weight, dst, num_segments=n)
        agg = agg / jnp.maximum(deg, 1.0)[:, None]
        h = x @ W_self + b_self + agg
        x1 = _layer_norm(x + h, ln1_g, ln1_b)
        ffn = jax.nn.gelu(x1 @ W_ffn1 + b_ffn1, approximate=False) @ W_ffn2 + b_ffn2
        out = _layer_norm(x1 + ffn, ln2_g, ln2_b)
        return out

    def _L2_gnn_ref(x, edge_index, weight, bias):
        import jax, jax.numpy as jnp
        import numpy as np
        N, E, D_IN, D_OUT = (512, 16384, 512, 512)
        support = x @ weight
        n = x.shape[0]
        adj = jnp.zeros((n, n), dtype=x.dtype).at[edge_index[0], edge_index[1]].set(1.0)
        adj = adj + jnp.eye(n, dtype=x.dtype)
        degree = adj.sum(axis=1, keepdims=True)
        d_inv_sqrt = jnp.where(degree > 0, jax.lax.rsqrt(degree), 0.0)
        adj_normalized = d_inv_sqrt * adj * d_inv_sqrt.T
        out = adj_normalized @ support + bias
        return out

    def _L3_gnn_ref(x, edge_index, Wl1, bl1, Wr1, Wl2, bl2, Wr2):
        import jax, jax.numpy as jnp
        import numpy as np
        N_NODES = 625
        N_EDGES = 10000
        D = 512

        def _sage_conv(x, src, dst, Wl, bl, Wr, num_nodes):
            msg = x[src]
            agg = jax.ops.segment_sum(msg, dst, num_segments=num_nodes)
            cnt = jax.ops.segment_sum(jnp.ones((src.shape[0],), x.dtype), dst, num_segments=num_nodes)
            agg = agg / jnp.maximum(cnt, 1.0)[:, None]
            return agg @ Wl.T + bl + x @ Wr.T
        src, dst = (edge_index[0], edge_index[1])
        num_nodes = x.shape[0]
        h = jax.nn.relu(_sage_conv(x, src, dst, Wl1, bl1, Wr1, num_nodes))
        return _sage_conv(h, src, dst, Wl2, bl2, Wr2, num_nodes)
    edge_index = jnp.stack([src, dst])
    h = jnp.maximum(_layernorm(x, axis=-1), 0.0)
    x = x + _L0_gnn_ref(h, edge_index, L0_gnn_W, L0_gnn_b, L0_gnn_diffusion_weights)
    h = jnp.maximum(_layernorm(x, axis=-1), 0.0)
    x = x + _L1_gnn_ref(h, edge_index, edge_type_4, edge_weight, L1_gnn_W_self, L1_gnn_b_self, L1_gnn_W_rel, L1_gnn_b_rel, L1_gnn_ln1_g, L1_gnn_ln1_b, L1_gnn_ln2_g, L1_gnn_ln2_b, L1_gnn_W_ffn1, L1_gnn_b_ffn1, L1_gnn_W_ffn2, L1_gnn_b_ffn2)
    h = jnp.maximum(_layernorm(x, axis=-1), 0.0)
    x = x + _L2_gnn_ref(h, edge_index, L2_gnn_weight, L2_gnn_bias)
    h = jnp.maximum(_layernorm(x, axis=-1), 0.0)
    x = x + _L3_gnn_ref(h, edge_index, L3_gnn_Wl1, L3_gnn_bl1, L3_gnn_Wr1, L3_gnn_Wl2, L3_gnn_bl2, L3_gnn_Wr2)
    return x

_drawn_inputs = setup_inputs


def setup_inputs(seed=0):
    import zlib

    import numpy as np

    out = dict(_drawn_inputs(seed))
    spreads = {'L0_gnn_b': (0.0, 0.1),
     'L0_gnn_diffusion_weights': (0.25, 0.6),
     'L1_gnn_b_self': (0.0, 0.1),
     'L1_gnn_b_rel': (0.0, 0.1),
     'L1_gnn_ln1_g': (1.0, 0.2),
     'L1_gnn_ln1_b': (0.0, 0.1),
     'L1_gnn_ln2_g': (1.0, 0.2),
     'L1_gnn_ln2_b': (0.0, 0.1),
     'L1_gnn_b_ffn1': (0.0, 0.449),
     'L1_gnn_b_ffn2': (0.0, 0.1),
     'L2_gnn_bias': (0.0, 0.1)}
    factors = {'L3_gnn_bl1': 7.945, 'L3_gnn_bl2': 4.455}
    for name, (base, spread) in spreads.items():
        noise = np.random.default_rng([zlib.crc32(name.encode()), seed]).standard_normal(out[name].shape)
        drawn = base * np.exp(spread * noise) if base else spread * noise
        out[name] = jnp.asarray(drawn.astype(out[name].dtype))
    for name, factor in factors.items():
        out[name] = (out[name] * factor).astype(out[name].dtype)
    return out
```

```python
from contextlib import ExitStack

import concourse.bass as bass
from concourse import mybir

F32 = mybir.dt.float32
F32R = mybir.dt.float32r
BF16 = mybir.dt.bfloat16
F16 = mybir.dt.float16
I32 = mybir.dt.int32
ALU = mybir.AluOpType
ACT = mybir.ActivationFunctionType
AX = mybir.AxisListType
PE, DVE = mybir.EngineType.PE, mybir.EngineType.DVE

P = 128
N = 512
D = 512
E = 16384
R = 4
NT = N // P
KT = D // P
CH = E // P
WD = 8
NW = N // WD
WC = 4
V = 4
WK = R * WD
OUT_R = R + 1
UNROLL = 8
GROUP = 4
F1 = 2 * D
GT = F1 // P
EPS = 1e-5
HOPS = 3
assert N == D and V * WK == P and NW % UNROLL == 0 and E % P == 0


def gnn_program(nc, x_in, src_in, dst_in, typ_in, wgt_in, w0_in, b0_in, dw_in, wself_in, bself_in, wrel_in, brel_in,
                g1_in, be1_in, g2_in, be2_in, wf1_in, bf1_in, wf2_in, bf2_in, w2_in, b2_in,
                wl1_in, bl1_in, wr1_in, wl2_in, bl2_in, wr2_in, out):
    with ExitStack() as keep:
        def sem(name):
            return keep.enter_context(nc.semaphore(name))

        def sb(name, shape, dt):
            return keep.enter_context(nc.sbuf_tensor(name, shape, dt))

        wall = sb("wall", [P, NT, OUT_R, N], F32)
        x = sb("x", [P, NT, D], F32)
        ident = sb("ident", [P, P], F32)
        ones = sb("ones", [P, P], F32)
        psum = [keep.enter_context(nc.psum_tensor(f"bank{i}", [P, 512], F32)) for i in range(8)]
        x_loaded = sem("x_loaded")
        build_matrices(nc, sem, wall, x, ident, ones, psum, x_loaded, x_in, src_in, dst_in, typ_in, wgt_in)
        run_blocks(nc, sem, wall, x, ident, ones, psum, x_loaded, w0_in, b0_in, dw_in, wself_in, bself_in, wrel_in,
                   brel_in, g1_in, be1_in, g2_in, be2_in, wf1_in, bf1_in, wf2_in, bf2_in, w2_in, b2_in,
                   wl1_in, bl1_in, wr1_in, wl2_in, bl2_in, wr2_in, out)


def build_matrices(nc, sem, wall, x, ident, ones, psum, x_loaded, x_in, src_in, dst_in, typ_in, wgt_in):
    with ExitStack() as ctx:
        def sb(name, shape, dt):
            return ctx.enter_context(nc.sbuf_tensor(name, shape, dt))

        src_hot = sb("src_hot", [P, CH, N], BF16)
        e_int = sb("e_int", [P, 3, P], I32)
        e_wgt = sb("e_wgt", [P, P], F32)
        e_f32 = sb("e_f32", [P, 3, P], F32)
        next_dst_i = sb("next_dst_i", [P, 1], I32)
        next_dst = sb("next_dst", [P, 1], F32)
        key_t = sb("key_t", [P, CH], F32)
        src_t = sb("src_t", [P, CH], F32)
        wgt_t = sb("wgt_t", [P, CH], F32)
        rest = sb("rest", [P, 2, CH], F32)
        part_b = sb("part_b", [P, 3, CH], BF16)
        parts = sb("parts", [P, CH, 3], F32)
        key_iota_i = wall[:, 0, 0:R, :].rearrange("p r n -> p (r n)").bitcast(I32)
        key_iota = sb("key_iota", [P, R, N], F16)
        win_lo = sb("win_lo", [P, NW], F32)
        chunk_cmp = sb("chunk_cmp", [P, 2, NW], F32)
        disorder = sb("disorder", [P, P], F32)
        viol = sb("viol", [P, 4], F32)
        span = sb("span", [P, 3, NW], F32)
        first_chunk = sb("first_chunk", [P, NW], I32)
        slow_flag = sb("slow_flag", [P, 1], I32)
        win = sb("win", [P, GROUP, WC, V, WK], BF16)
        z_sb = sb("z_sb", [P, 2, N], F32)
        fold = sb("fold", [P, OUT_R, WD], F32)
        slow_src, slow_key, zeros = src_hot[:, 0, :], src_hot[:, 1:1 + V, :], src_hot[:, 1 + V, :]

        dst_loaded, src_loaded, typ_loaded, wgt_loaded = (sem(f"{n}_loaded") for n in ("dst", "src", "typ", "wgt"))
        next_set, next_loaded = sem("next_set"), sem("next_loaded")
        const_set, const_ready = sem("const_set"), sem("const_ready")
        iota_ready = sem("iota_ready")
        edges_ready, edges_t_ready = sem("edges_ready"), sem("edges_t_ready")
        cmp_ready, cmp_sum_ready = sem("cmp_ready"), sem("cmp_sum_ready")
        viol_sum_ready, plan_ready = sem("viol_sum_ready"), sem("plan_ready")
        chain_sem = sem("build_chain")
        hot_ready = sem("hot_ready")
        win_hot, win_ready = sem("win_hot"), sem("win_ready")
        z_ready, z_copied, folded, wall_copied = sem("z_ready"), sem("z_copied"), sem("folded"), sem("wall_copied")
        slow_free, slow_ready, slow_sum, slow_out = sem("slow_free"), sem("slow_ready"), sem("slow_sum"), sem("slow_out")
        slow_cnt, slow_cnt_out, slow_zero = sem("slow_cnt"), sem("slow_cnt_out"), sem("slow_zero")

        z_bank = psum[0:2]
        out_bank = [psum[2:4], psum[4:6]]
        edge_bank, cmp_bank = psum[6], psum[7]
        chunked = "(c e) -> c e"

        block = ctx.enter_context(nc.Block())

        @block.sync
        def _(sp):
            sp.dma_start(e_int[:, 0, :], dst_in.rearrange(chunked, e=P)).then_inc(dst_loaded, 16)
            sp.wait_ge(next_set, 1)
            sp.dma_start(next_dst_i[0:CH - 1, :], dst_in.rearrange(chunked, e=P)[1:CH, 0:1],
                         allow_slow_non_contiguous=True).then_inc(next_loaded, 16)
            sp.dma_start(e_int[:, 2, :], typ_in.rearrange(chunked, e=P)).then_inc(typ_loaded, 16)
            sp.dma_start(x[:], x_in.rearrange("(t p) f -> p t f", p=P)).then_inc(x_loaded, 16)

        @block.gpsimd
        def _(pool):
            pool.memset(next_dst_i[:], N).then_inc(next_set, 1)
            pool.memset(ident[:], 0.0).then_inc(const_set, 1)
            pool.memset(fold[:], 0.0).then_inc(const_set, 1)
            pool.memset(ones[:], 1.0).then_inc(const_ready, 1)
            pool.wait_ge(const_set, 2)
            pool.affine_select(out=ident[:], in_=ident[:], compare_op=ALU.not_equal, fill=1.0, base=0,
                               pattern=[[-1, P]], channel_multiplier=1).then_inc(const_ready, 1)
            for v in range(V - 1):
                last = pool.affine_select(out=fold[:, 0:R, :], in_=fold[:, 0:R, :], compare_op=ALU.not_equal, fill=1.0,
                                          base=-WK * v, pattern=[[-WD, R], [-1, WD]], channel_multiplier=1)
                last.then_inc(const_set, 1)
                pool.wait_ge(const_set, 3 + v)
            for r in range(R):
                last = pool.affine_select(out=fold[:, R, :], in_=fold[:, R, :], compare_op=ALU.not_equal, fill=1.0,
                                          base=-WK * (V - 1) - WD * r, pattern=[[-1, WD]], channel_multiplier=1)
                last.then_inc(const_set, 1)
                pool.wait_ge(const_set, 2 + V + r)
            pool.iota(win_lo[:], pattern=[[WD, NW]], base=0, channel_multiplier=0,
                      allow_small_or_imprecise_dtypes=True).then_inc(const_ready, 1)
            pool.iota(key_iota_i, pattern=[[1, R * N]], base=0, channel_multiplier=0).then_inc(iota_ready, 1)
            pool.wait_ge(iota_ready, 1)
            pool.tensor_copy(key_iota[:].rearrange("p r n -> p (r n)"), key_iota_i).then_inc(iota_ready, 1)

        @block.scalar
        def _(act):
            act.dma_start(e_int[:, 1, :], src_in.rearrange(chunked, e=P)).then_inc(src_loaded, 16)
            act.dma_start(e_wgt[:], wgt_in.rearrange(chunked, e=P)).then_inc(wgt_loaded, 16)
            act.wait_ge(plan_ready, 2)
            slow = act.to_reg(nc.values_load_multi_w_load_instructions(
                slow_flag[0:1, 0:1], [mybir.EngineType.Activation], min_val=0, max_val=1,
                skip_runtime_bounds_check_because="the chip writes 0 or 1")[1][0])

            def copy_z(first, i):
                for j in range(UNROLL):
                    act.wait_ge(z_ready, i * UNROLL + j + 1)
                    if not (first and j < 2):
                        act.wait_ge(folded, i * UNROLL + j - 1)
                    act.activation(z_sb[:, j % 2, :], z_bank[j % 2][:], ACT.Copy).then_inc(z_copied, 1)

            with act.If_eq(slow, 0):
                copy_z(True, 0)
                with act.Fori(1, NW // UNROLL) as i:
                    copy_z(False, i)

        @block.vector
        def _(dve):
            links = [0]

            def link(ins):
                links[0] += 1
                ins.then_inc(chain_sem, 1)
                dve.wait_ge(chain_sem, links[0])

            dve.wait_ge(dst_loaded, 16)
            dve.tensor_copy(e_f32[:, 0, :], e_int[:, 0, :]).then_inc(edges_ready, 1)
            dve.wait_ge(src_loaded, 16)
            dve.tensor_copy(e_f32[:, 1, :], e_int[:, 1, :]).then_inc(edges_ready, 1)
            dve.wait_ge(typ_loaded, 16)
            dve.scalar_tensor_tensor(e_f32[:, 2, :], e_int[:, 2, :], float(N), e_int[:, 0, :], ALU.mult, ALU.add)\
                .then_inc(edges_ready, 1)
            dve.wait_ge(edges_ready, 1)
            dve.wait_ge(const_ready, 3)
            dve.tensor_scalar(chunk_cmp[:, 0, :], win_lo[:], e_f32[:, 0, P - 1:P], None, ALU.is_gt).then_inc(cmp_ready, 1)
            link(dve.tensor_scalar(span[:, 0, :], win_lo[:], float(WD), None, ALU.add))
            dve.tensor_scalar(chunk_cmp[:, 1, :], span[:, 0, :], e_f32[:, 0, 0:1], None, ALU.is_gt).then_inc(cmp_ready, 1)
            dve.wait_ge(next_loaded, 16)
            link(dve.tensor_copy(next_dst[:], next_dst_i[:]))
            dve.tensor_tensor(viol[:, 1:2], e_f32[:, 0, P - 1:P], next_dst[:], ALU.is_gt).then_inc(cmp_ready, 1)
            link(dve.tensor_tensor(disorder[:, 0:P - 1], e_f32[:, 0, 0:P - 1], e_f32[:, 0, 1:P], ALU.is_gt))
            dve.tensor_reduce(viol[:, 0:1], disorder[:, 0:P - 1], AX.X, ALU.add).then_inc(cmp_ready, 1)

            dve.wait_ge(edges_t_ready, 3)
            dve.tensor_copy(src_t[:], edge_bank[:, 0:P]).then_inc(edges_ready, 1)
            dve.tensor_copy(key_t[:], edge_bank[:, P:2 * P]).then_inc(edges_ready, 1)
            link(dve.tensor_copy(wgt_t[:], edge_bank[:, 2 * P:3 * P]))
            link(dve.tensor_copy(part_b[:, 0, :], wgt_t[:]))
            link(dve.tensor_tensor(rest[:, 0, :], wgt_t[:], part_b[:, 0, :], ALU.subtract))
            link(dve.tensor_copy(part_b[:, 1, :], rest[:, 0, :]))
            link(dve.tensor_tensor(rest[:, 1, :], rest[:, 0, :], part_b[:, 1, :], ALU.subtract))
            link(dve.tensor_copy(part_b[:, 2, :], rest[:, 1, :]))
            link(dve.tensor_copy(parts[:].rearrange("p c v -> p v c"), part_b[:]))

            dve.wait_ge(cmp_sum_ready, 1)
            link(dve.tensor_scalar(span[:, 0, :], cmp_bank[:, 0:NW], float(CH - WC), None, ALU.min))
            dve.tensor_copy(first_chunk[:], span[:, 0, :]).then_inc(plan_ready, 1)
            link(dve.tensor_tensor(span[:, 1, :], cmp_bank[:, NW:2 * NW], span[:, 0, :], ALU.subtract))
            link(dve.tensor_scalar(span[:, 2, :], span[:, 1, :], float(WC), None, ALU.is_gt))
            link(dve.tensor_reduce(viol[:, 2:3], span[:, 2, :], AX.X, ALU.add))
            dve.tensor_copy(viol[:, 3:4], cmp_bank[:, 2 * NW:2 * NW + 1]).then_inc(chain_sem, 1)
            links[0] += 1
            dve.wait_ge(chain_sem, links[0])
            link(dve.tensor_tensor(span[:, 1, 0:1], viol[:, 2:3], viol[:, 3:4], ALU.add))
            dve.tensor_scalar(slow_flag[:], span[:, 1, 0:1], 0.0, None, ALU.is_gt).then_inc(plan_ready, 1)
            dve.wait_ge(plan_ready, 2)
            slow = dve.to_reg(nc.values_load_multi_w_load_instructions(
                slow_flag[0:1, 0:1], [DVE], min_val=0, max_val=1,
                skip_runtime_bounds_check_because="the chip writes 0 or 1")[1][0])
            dve.wait_ge(iota_ready, 2)
            dve.wait_ge(edges_ready, 5)

            def windows(first, i):
                starts = nc.values_load_multi_w_load_instructions(
                    first_chunk[0:1, bass.ds(i * UNROLL, UNROLL)], [DVE], min_val=0, max_val=CH - WC,
                    skip_runtime_bounds_check_because="clamped to that on the chip")[1]
                for j0 in range(0, UNROLL, GROUP):
                    for j in range(j0, j0 + GROUP):
                        if not (first and j < GROUP):
                            dve.wait_ge(z_ready, i * UNROLL + j - GROUP + 1)
                        key = key_t[:, bass.ds(starts[j], WC)].unsqueeze(2).unsqueeze(3).broadcast_to([P, WC, R, WD])
                        want = key_iota[:, :, bass.ds((i * UNROLL + j) * WD, WD)].unsqueeze(1).broadcast_to([P, WC, R, WD])
                        dve.tensor_tensor(win[:, j % GROUP, :, V - 1, :].rearrange("p c (r d) -> p c r d", r=R),
                                          key, want, ALU.is_equal).then_inc(win_hot, 1)
                    for j in range(j0, j0 + GROUP):
                        dve.wait_ge(win_hot, i * UNROLL + j + 1)
                        hot = win[:, j % GROUP, :, V - 1, :].unsqueeze(2).broadcast_to([P, WC, V - 1, WK])
                        wgt = parts[:, bass.ds(starts[j], WC), :].unsqueeze(3).broadcast_to([P, WC, V - 1, WK])
                        dve.tensor_tensor(win[:, j % GROUP, :, 0:V - 1, :], hot, wgt, ALU.mult).then_inc(win_ready, 1)
                    if not (first and j0 == 0):
                        copy_out(i * UNROLL + j0 - GROUP, (j0 // GROUP + 1) % 2)

            def copy_out(w0, side):
                dve.wait_ge(folded, w0 + GROUP)
                for half in range(2):
                    got = out_bank[side][half][:, 0:2 * OUT_R * GROUP * WD].rearrange("p (t r d) -> p t r d", t=2, r=OUT_R)
                    dve.tensor_copy(wall[:, 2 * half:2 * half + 2, :, bass.ds(w0 * WD, GROUP * WD)], got)\
                        .then_inc(wall_copied, 1)

            with dve.If_eq(slow, 0):
                for c in range(CH):
                    dve.tensor_scalar(src_hot[:, c, :], key_iota[:, 0, :], src_t[:, c:c + 1], None, ALU.is_equal)\
                        .then_inc(hot_ready, 1)
                windows(True, 0)
                with dve.Fori(1, NW // UNROLL) as i:
                    windows(False, i)
                copy_out(NW - GROUP, 1)

            with dve.If_ne(slow, 0):
                dve.memset(zeros, 0.0).then_inc(slow_zero, 1)
                dve.memset(slow_src, 0.0).then_inc(slow_free, 1)
                with dve.Fori(0, R) as r:
                    with dve.Fori(0, CH) as c:
                        dve.wait_ge(slow_free, r * CH + c + 1)
                        dve.tensor_scalar(slow_src, key_iota[:, 0, :], src_t[:, bass.ds(c, 1)], None, ALU.is_equal)\
                            .then_inc(slow_ready, 1)
                        for v in range(V - 1):
                            dve.tensor_scalar(slow_key[:, v, :], key_iota[:, bass.ds(r, 1), :].squeeze(1),
                                              key_t[:, bass.ds(c, 1)], parts[:, bass.ds(c, 1), v], ALU.is_equal, ALU.mult)\
                                .then_inc(slow_ready, 1)
                        dve.tensor_scalar(slow_key[:, V - 1, :], key_iota[:, bass.ds(r, 1), :].squeeze(1),
                                          key_t[:, bass.ds(c, 1)], None, ALU.is_equal).then_inc(slow_ready, 1)
                    dve.wait_ge(slow_sum, r + 1)
                    for t in range(NT):
                        dve.tensor_copy(wall[:, t, bass.ds(r, 1), :].squeeze(1), psum[t][:]).then_inc(slow_out, 1)
                dve.wait_ge(slow_cnt, 1)
                for t in range(NT):
                    dve.tensor_copy(wall[:, t, R, :], psum[NT + t][:]).then_inc(slow_cnt_out, 1)

        @block.tensor
        def _(pe):
            pe.wait_ge(const_ready, 3)
            pe.wait_ge(edges_ready, 2)
            pe.transpose(edge_bank[:, 0:P], e_f32[:, 1, :], ident[:]).then_inc(edges_t_ready, 1)
            pe.wait_ge(edges_ready, 3)
            pe.transpose(edge_bank[:, P:2 * P], e_f32[:, 2, :], ident[:]).then_inc(edges_t_ready, 1)
            pe.wait_ge(wgt_loaded, 16)
            pe.transpose(edge_bank[:, 2 * P:3 * P], e_wgt[:], ident[:]).then_inc(edges_t_ready, 1)
            pe.wait_ge(cmp_ready, 4)
            pe.matmul(cmp_bank[:, 0:2 * NW], ones[:], chunk_cmp[:].rearrange("p a w -> p (a w)"), start=True, stop=True)
            pe.matmul(cmp_bank[:, 2 * NW:2 * NW + 1], ones[:], viol[:, 0:1], start=False, stop=False, skip_group_check=True)
            pe.matmul(cmp_bank[:, 2 * NW:2 * NW + 1], ones[:], viol[:, 1:2], start=False, stop=True, skip_group_check=True)\
                .then_inc(cmp_sum_ready, 1)
            pe.wait_ge(plan_ready, 2)
            slow = pe.to_reg(nc.values_load_multi_w_load_instructions(
                slow_flag[0:1, 0:1], [PE], min_val=0, max_val=1,
                skip_runtime_bounds_check_because="the chip writes 0 or 1")[1][0])

            def fold_window(w, j):
                pe.wait_ge(z_copied, w + 1)
                side = out_bank[(j // GROUP) % 2]
                for t in range(NT):
                    col = (t % 2) * OUT_R * GROUP * WD
                    to = side[t // 2][:, col:col + OUT_R * GROUP * WD].rearrange("p (r w d) -> p r w d", r=OUT_R, w=GROUP)
                    ins = pe.matmul(to[:, :, j % GROUP, :], z_sb[:, j % 2, t * P:(t + 1) * P], fold[:],
                                    start=True, stop=True)
                ins.then_inc(folded, 1)

            def sum_windows(first, i):
                starts = nc.values_load_multi_w_load_instructions(
                    first_chunk[0:1, bass.ds(i * UNROLL, UNROLL)], [PE], min_val=0, max_val=CH - WC,
                    skip_runtime_bounds_check_because="clamped to that on the chip")[1]
                for j in range(UNROLL):
                    pe.wait_ge(win_ready, i * UNROLL + j + 1)
                    if not (first and j < 2):
                        pe.wait_ge(z_copied, i * UNROLL + j - 1)
                    for c in range(WC):
                        ins = pe.matmul(z_bank[j % 2][:], win[:, j % GROUP, c, :, :].rearrange("p v k -> p (v k)"),
                                        src_hot[:, bass.ds(starts[j] + c, 1), :].squeeze(1), start=(c == 0), stop=(c == WC - 1))
                    ins.then_inc(z_ready, 1)
                    if first and j == 0:
                        continue
                    if (j - 1) % GROUP == 0 and not (first and j - 1 < 2 * GROUP):
                        pe.wait_ge(wall_copied, i * (2 * UNROLL // GROUP) + 2 * ((j - 1) // GROUP) - 2)
                    fold_window(i * UNROLL + j - 1, (j - 1) % UNROLL)

            with pe.If_eq(slow, 0):
                pe.wait_ge(hot_ready, CH)
                sum_windows(True, 0)
                with pe.Fori(1, NW // UNROLL) as i:
                    sum_windows(False, i)
                fold_window(NW - 1, UNROLL - 1)

            with pe.If_ne(slow, 0):
                pe.wait_ge(slow_zero, 1)
                for t in range(NT):
                    pe.matmul(psum[NT + t][:], zeros[:, 0:P], zeros, start=True, stop=False)
                with pe.Fori(0, R) as r:
                    for t in range(NT):
                        pe.matmul(psum[t][:], zeros[:, 0:P], zeros, start=True, stop=False)
                    with pe.Fori(0, CH) as c:
                        pe.wait_ge(slow_ready, (r * CH + c + 1) * (V + 1))
                        for t in range(NT):
                            for v in range(V - 1):
                                pe.matmul(psum[t][:], slow_src[:, t * P:(t + 1) * P], slow_key[:, v, :], start=False, stop=False)
                            ins = pe.matmul(psum[NT + t][:], slow_src[:, t * P:(t + 1) * P], slow_key[:, V - 1, :],
                                            start=False, stop=False)
                        ins.then_inc(slow_free, 1)
                    for t in range(NT):
                        ins = pe.matmul(psum[t][:], zeros[:, 0:P], zeros, start=False, stop=True)
                    ins.then_inc(slow_sum, 1)
                    pe.wait_ge(slow_out, r * NT + NT)
                for t in range(NT):
                    ins = pe.matmul(psum[NT + t][:], zeros[:, 0:P], zeros, start=False, stop=True)
                ins.then_inc(slow_cnt, 1)


H0, H1, H2, WL1, H3, WR1, WL2, H4, WR2, H5 = range(10)


def use_of(what, t):
    return NT * what + t


def run_blocks(nc, sem, wall, x, ident, ones, psum, x_loaded, w0_in, b0_in, dw_in, wself_in, bself_in, wrel_in, brel_in,
               g1_in, be1_in, g2_in, be2_in, wf1_in, bf1_in, wf2_in, bf2_in, w2_in, b2_in,
               wl1_in, bl1_in, wr1_in, wl2_in, bl2_in, wr2_in, out):
    with ExitStack() as ctx:
        def sb(name, shape, dt):
            return ctx.enter_context(nc.sbuf_tensor(name, shape, dt))

        slots = sb("slots", [P, 8, KT * D], F32)

        def place(n, k=KT):
            return slots[:, n:n + k // KT, :].rearrange("p a (k n) -> p (a k) n", k=KT)

        w0, wself, wrel = place(0), place(1), [place(2 + r) for r in range(R)]
        msg = [place(6), place(7), place(0), place(1)]
        wgt_sum = place(7)
        wf1 = slots[:, 2:4, :].rearrange("p a n -> p (a n)").rearrange("p (k n) -> p k n", k=KT)
        wf2 = place(4, GT)
        hid = place(6, GT)
        w2 = place(0)
        sage_raw = [place(1), place(2), place(3), place(4)]
        agg_t = [place(6), place(7)]

        def sage(q, k):
            return wall[:, k, q, :]

        count = [wall[:, t, R, :] for t in range(NT)]
        h = sb("h", [P, NT, D], F32)
        h_t = sb("h_t", [P, KT, N], F32)
        adj = sb("adj", [P, NT, N], F32R)
        hi = [sb(f"hi{i}", [P, NT, D], F32R) for i in range(2)]
        lo = [sb(f"lo{i}", [P, NT, D], F32R) for i in range(2)]
        cur = sb("cur", [P, 2, D], F32)
        eye = sb("eye", [P, 2 * N - P], F32)
        bias = sb("bias", [P, 11, D], F32)
        b0, bself, g1, be1, g2, be2, bf2 = (bias[:, i, :] for i in range(7))
        brel = [bias[:, 7 + r, :] for r in range(R)]
        b2, bl1, bl2 = (bias[:, 7 + i, :] for i in range(3))
        bf1 = sb("bf1", [P, GT], F32)
        dw = sb("dw", [P, HOPS + 1], F32)
        dw_inv = sb("dw_inv", [P, HOPS, NT], F32)
        eps = sb("eps", [P, 1], F32)
        stats = sb("stats", [P, NT, 6], F32)
        mean_var = sb("mean_var", [P, NT, 2], F32)
        std = sb("std", [P, NT], F32)
        rstd = sb("rstd", [P, NT], F32)
        shift = sb("shift", [P, NT], F32)
        row_sum = sb("row_sum", [P, NT], F32)
        inv_row = sb("inv_row", [P, NT], F32)
        out_deg = sb("out_deg", [P, NT], F32)
        deg_root = sb("deg_root", [P, NT], F32)
        inv_root = sb("inv_root", [P, NT], F32)
        wgt_deg = sb("wgt_deg", [P, NT], F32)
        inv_wgt = sb("inv_wgt", [P, NT], F32)
        inv_cnt = sb("inv_cnt", [P, N], F32)

        rows_loaded, rel_rows_loaded, late_rows_loaded = sem("rows_loaded"), sem("rel_rows_loaded"), sem("late_rows_loaded")
        dw_loaded, bf1_loaded = sem("dw_loaded"), sem("bf1_loaded")
        w0_loaded, wself_loaded, w2_loaded = sem("w0_loaded"), sem("wself_loaded"), sem("w2_loaded")
        wrel_loaded = [sem(f"wrel{r}_loaded") for r in range(R)]
        wf1_loaded, wf2_loaded = sem("wf1_loaded"), sem("wf2_loaded")
        sage_loaded = [sem(f"sage{q}_loaded") for q in range(4)]
        out_stored = sem("out_stored")
        eye_set, eye_ready, eps_ready = sem("eye_set"), sem("eye_ready"), sem("eps_ready")
        wgt_add, self_biased, ffn_biased, ln2_biased = sem("wgt_add"), sem("self_biased"), sem("ffn_biased"), sem("ln2_biased")
        gcn_biased, sage_biased = sem("gcn_biased"), sem("sage_biased")
        NORMS = 6
        var_ready = [sem(f"var_ready{n}") for n in range(NORMS)]
        std_ready = [sem(f"std_ready{n}") for n in range(NORMS)]
        shift_ready = [sem(f"shift_ready{n}") for n in range(NORMS)]
        h_ready = [sem(f"h_ready{n}") for n in range(NORMS)]
        t_ready, t_out = sem("t_ready"), sem("t_out")
        cnt_ready, cnt_out, cnt_t_ready, cnt_t_out = sem("cnt_ready"), sem("cnt_out"), sem("cnt_t_ready"), sem("cnt_t_out")
        inv_row_ready, deg_ready, deg_root_ready, wgt_deg_ready, wgt_deg_out = (
            sem("inv_row_ready"), sem("deg_ready"), sem("deg_root_ready"), sem("wgt_deg_ready"), sem("wgt_deg_out"))
        gcn_adj_ready = sem("gcn_adj_ready")
        proj_ready, proj_out, hi_ready, lo_ready, acc_ready = (
            sem("proj_ready"), sem("proj_out"), sem("hi_ready"), sem("lo_ready"), sem("acc_ready"))
        hop_ready, hop_out, diff_done = sem("hop_ready"), sem("hop_out"), sem("diff_done")
        self_ready, self_out, msg_ready, msg_out, agg_ready, agg_out = (
            sem("self_ready"), sem("self_out"), sem("msg_ready"), sem("msg_out"), sem("agg_ready"), sem("agg_out"))
        up_ready, up_out, down_ready, down_out = sem("up_ready"), sem("up_out"), sem("down_ready"), sem("down_out")
        ln_mid, ln2_done = sem("ln_mid"), sem("ln2_done")
        sup_ready, sup_out, sup_hi, gcn_ready, gcn_out = (
            sem("sup_ready"), sem("sup_out"), sem("sup_hi"), sem("gcn_ready"), sem("gcn_out"))
        mean_ready, mean_out = [sem(f"mean_ready{i}") for i in range(2)], [sem(f"mean_out{i}") for i in range(2)]
        sage_ready, sage_out = [sem(f"sage_ready{i}") for i in range(2)], [sem(f"sage_out{i}") for i in range(2)]
        relu_ready = sem("relu_ready")
        chain_sem = sem("run_chain")

        main, t_bank, cnt_bank, misc_bank = psum[0:4], psum[4:6], psum[6], psum[7]
        HALF = N // 2

        def row(ap):
            return ap.partition_broadcast(P)

        def tiled(ap, p=P):
            return ap.rearrange("(k p) n -> p k n", p=p)

        block = ctx.enter_context(nc.Block())

        @block.sync
        def _(sp):
            sp.dma_start(w0, tiled(w0_in)).then_inc(w0_loaded, 16)
            sp.dma_start(wself, tiled(wself_in)).then_inc(wself_loaded, 16)
            for r in range(R):
                sp.dma_start(wrel[r], tiled(wrel_in[r])).then_inc(wrel_loaded[r], 16)
            sp.wait_ge(msg_ready, R * NT)
            sp.dma_start(wf1, tiled(wf1_in)).then_inc(wf1_loaded, 16)
            sp.dma_start(wf2, tiled(wf2_in)).then_inc(wf2_loaded, 16)
            sp.wait_ge(agg_ready, NT)
            sp.dma_start(sage_raw[0], tiled(wl1_in)).then_inc(sage_loaded[0], 16)
            sp.dma_start(w2, tiled(w2_in)).then_inc(w2_loaded, 16)
            sp.wait_ge(up_ready, GT)
            sp.dma_start(sage_raw[1], tiled(wr1_in)).then_inc(sage_loaded[1], 16)
            sp.dma_start(sage_raw[2], tiled(wl2_in)).then_inc(sage_loaded[2], 16)
            sp.wait_ge(down_ready, NT)
            sp.dma_start(sage_raw[3], tiled(wr2_in)).then_inc(sage_loaded[3], 16)
            for m in range(NT):
                sp.wait_ge(sage_out[1], m + 1)
                sp.dma_start(out[m * P:(m + 1) * P, :], x[:, m, :]).then_inc(out_stored, 16)
            sp.wait_ge(out_stored, 16 * NT)

        @block.gpsimd
        def _(pool):
            pool.dma_start(b0, row(b0_in)).then_inc(rows_loaded, 16)
            pool.dma_start(dw[:], row(dw_in)).then_inc(dw_loaded, 16)
            for to, of in ((bself, bself_in), (g1, g1_in), (be1, be1_in), (g2, g2_in), (be2, be2_in), (bf2, bf2_in)):
                pool.dma_start(to, row(of)).then_inc(rows_loaded, 16)
            for r in range(R):
                pool.dma_start(brel[r], row(brel_in[r])).then_inc(rel_rows_loaded, 16)
            pool.dma_start(bf1[:], bf1_in.rearrange("(g p) -> p g", p=P), allow_slow_non_contiguous=True).then_inc(bf1_loaded, 16)
            pool.memset(eps[:], EPS).then_inc(eps_ready, 1)
            pool.memset(eye[:], 0.0).then_inc(eye_set, 1)
            pool.wait_ge(eye_set, 1)
            pool.affine_select(out=eye[:], in_=eye[:], compare_op=ALU.not_equal, fill=1.0, base=N - P,
                               pattern=[[-1, 2 * N - P]], channel_multiplier=1).then_inc(eye_ready, 1)
            pool.tensor_tensor(wgt_sum, wall[:, :, 0, :], wall[:, :, 1, :], ALU.add).then_inc(wgt_add, 1)
            for r in range(2, R):
                pool.wait_ge(wgt_add, r - 1)
                pool.tensor_tensor(wgt_sum, wgt_sum, wall[:, :, r, :], ALU.add).then_inc(wgt_add, 1)
            pool.wait_ge(rows_loaded, 16 * 7)
            for t in range(NT):
                pool.wait_ge(t_ready, use_of(H1, t) + 1)
                pool.tensor_tensor(h[:, t, :], h[:, t, :], bself, ALU.add).then_inc(self_biased, 1)
                pool.wait_ge(h_ready[1], t + 1)
                pool.tensor_tensor(x[:, t, :], x[:, t, :], be2, ALU.add).then_inc(ln2_biased, 1)
            pool.wait_ge(msg_out, R * NT)
            for to, of in ((b2, b2_in), (bl1, bl1_in), (bl2, bl2_in)):
                pool.dma_start(to, row(of)).then_inc(late_rows_loaded, 16)
            for t in range(NT):
                pool.wait_ge(t_ready, use_of(H2, t) + 1)
                pool.tensor_tensor(h[:, t, :], h[:, t, :], bf2, ALU.add).then_inc(ffn_biased, 1)
            pool.wait_ge(late_rows_loaded, 16 * 3)
            for t in range(NT):
                pool.wait_ge(h_ready[4], t + 1)
                pool.tensor_tensor(x[:, t, :], x[:, t, :], b2, ALU.add).then_inc(gcn_biased, 1)
            for t in range(NT):
                pool.wait_ge(h_ready[5], t + 1)
                pool.tensor_tensor(x[:, t, :], x[:, t, :], bl2, ALU.add).then_inc(sage_biased, 1)

        @block.scalar
        def _(act):
            def root(n, t):
                act.wait_ge(var_ready[n], t + 1)
                act.activation(std[:, t:t + 1], mean_var[:, t, 1:2], ACT.Sqrt, bias=eps[:]).then_inc(std_ready[n], 1)

            def norm_relu(n, t):
                act.wait_ge(shift_ready[n], t + 1)
                act.activation(h[:, t, :], x[:, t, :], ACT.Relu, bias=shift[:, t:t + 1], scale=rstd[:, t:t + 1])\
                    .then_inc(h_ready[n], 1)

            def empty(use, to):
                act.wait_ge(t_ready, use + 1)
                act.activation(to, t_bank[use % 2][:].rearrange("p (a n) -> p a n", n=to.shape[-1]) if len(to.shape) == 3
                               else t_bank[use % 2][:], ACT.Copy).then_inc(t_out, 1)

            def empty_h(what, t):
                empty(use_of(what, t), h_t[:, :, t * P:(t + 1) * P])

            def empty_sage(what, q, k):
                empty(use_of(what, k), sage(q, k))

            def norm_and_transposes(n, what):
                for t in range(NT):
                    root(n, t)
                    norm_relu(n, t)
                    if t > 0:
                        empty_h(what, t - 1)
                empty_h(what, NT - 1)

            act.wait_ge(eps_ready, 1)
            norm_and_transposes(0, H0)
            for m in range(NT):
                act.wait_ge(proj_out, m + 1)
                act.activation(hi[0][:, m, :], cur[:, m % 2, :], ACT.Copy).then_inc(hi_ready, 1)
            act.wait_ge(deg_ready, 1)
            act.activation(deg_root[:], out_deg[:], ACT.Sqrt).then_inc(deg_root_ready, 1)
            act.wait_ge(inv_row_ready, 1)
            for i in range(1, HOPS):
                for m in range(NT):
                    act.wait_ge(hop_ready, (i - 1) * NT + m + 1)
                    act.activation(hi[i % 2][:, m, :], main[m][:], ACT.Copy, scale=inv_row[:, m:m + 1]).then_inc(hi_ready, 1)
            norm_and_transposes(1, H1)
            for t in range(NT):
                root(2, t)
                if t > 0:
                    empty_h(H2, t - 1)
            empty_h(H2, NT - 1)
            act.wait_ge(bf1_loaded, 16)
            for g in range(GT):
                act.wait_ge(up_ready, g + 1)
                act.activation(hid[:, g, :], main[g % 4][:], ACT.Gelu, bias=bf1[:, g:g + 1]).then_inc(up_out, 1)
            for t in range(NT):
                empty_sage(WL1, 0, t)
                root(3, t)
                root(4, t)
                norm_relu(4, t)
            for t in range(NT):
                empty_h(H3, t)
            for m in range(NT):
                act.wait_ge(sup_ready, m + 1)
                act.activation(hi[0][:, m, :], main[m][:], ACT.Copy, scale=inv_root[:, m:m + 1]).then_inc(sup_hi, 1)
                empty_sage(WR1, 1, m)
            for t in range(NT):
                empty_sage(WL2, 2, t)
                root(5, t)
                norm_relu(5, t)
            for t in range(NT):
                empty_h(H4, t)
            for k in range(KT):
                empty_sage(WR2, 3, k)
            for t in range(NT):
                act.wait_ge(sage_out[0], t + 1)
                act.activation(h[:, t, :], h[:, t, :], ACT.Relu).then_inc(relu_ready, 1)
                if t > 0:
                    empty_h(H5, t - 1)
            empty_h(H5, NT - 1)

        @block.vector
        def _(dve):
            links = [0]

            def link(ins):
                links[0] += 1
                ins.then_inc(chain_sem, 1)
                dve.wait_ge(chain_sem, links[0])

            def moments(n, t, rows):
                link(dve.bn_stats(stats[:, t, :], rows))
                dve.bn_aggr(mean_var[:, t, :], stats[:, t, :]).then_inc(var_ready[n], 1)

            def inverse_std(n, t):
                dve.wait_ge(std_ready[n], t + 1)
                link(dve.reciprocal(rstd[:, t:t + 1], std[:, t:t + 1]))

            def scale_and_shift(n, t):
                inverse_std(n, t)
                dve.tensor_scalar(shift[:, t:t + 1], mean_var[:, t, 0:1], rstd[:, t:t + 1], -1.0, ALU.mult, ALU.mult)\
                    .then_inc(shift_ready[n], 1)

            def affine_norm(n, t, rows, gain, plus, to):
                inverse_std(n, t)
                link(dve.scalar_tensor_tensor(rows, rows, mean_var[:, t, 0:1], gain, ALU.subtract, ALU.mult))
                return dve.scalar_tensor_tensor(to, rows, rstd[:, t:t + 1], plus, ALU.mult, ALU.add)

            def eye_of(t):
                return eye[:, N - P - t * P:2 * N - P - t * P]

            dve.wait_ge(x_loaded, 16)
            for t in range(NT):
                moments(0, t, x[:, t, :])
            dve.wait_ge(eye_ready, 1)
            for t in range(NT):
                scale_and_shift(0, t)
                dve.wait_ge(cnt_t_ready, t + 1)
                half = misc_bank if t % 2 else cnt_bank
                link(dve.tensor_tensor(cur[:, t % 2, :], half[:], count[t], ALU.add))
                dve.scalar_tensor_tensor(adj[:, t, :], cur[:, t % 2, :], 0.0, eye_of(t), ALU.is_gt, ALU.add,
                                         accum_out=row_sum[:, t:t + 1]).then_inc(cnt_t_out, 1)
            dve.wait_ge(cnt_t_out, NT)
            link(dve.tensor_scalar(inv_row[:], row_sum[:], 1.0, None, ALU.max))
            dve.reciprocal(inv_row[:], inv_row[:]).then_inc(inv_row_ready, 1)
            dve.wait_ge(dw_loaded, 16)
            dve.wait_ge(inv_row_ready, 1)
            for i in range(HOPS):
                link(dve.tensor_scalar(dw_inv[:, i, :], inv_row[:], dw[:, i + 1:i + 2], None, ALU.mult))
            dve.wait_ge(rows_loaded, 16 * 7)
            for m in range(NT):
                dve.wait_ge(proj_ready, m + 1)
                if m >= 2:
                    dve.wait_ge(lo_ready, m - 1)
                    dve.wait_ge(acc_ready, m - 1)
                dve.tensor_tensor(cur[:, m % 2, :], main[m][:], b0, ALU.add).then_inc(proj_out, 1)
                dve.wait_ge(proj_out, m + 1)
                dve.tensor_scalar(h[:, m, :], cur[:, m % 2, :], dw[:, 0:1], None, ALU.mult).then_inc(acc_ready, 1)
                dve.wait_ge(hi_ready, m + 1)
                dve.tensor_tensor(lo[0][:, m, :], cur[:, m % 2, :], hi[0][:, m, :].bitcast(F32), ALU.subtract)\
                    .then_inc(lo_ready, 1)
            for t in range(NT):
                link(dve.tensor_scalar(cur[:, t % 2, :], count[t], 0.0, None, ALU.is_gt))
                link(dve.tensor_reduce(out_deg[:, t:t + 1], cur[:, t % 2, :], AX.X, ALU.add))
            dve.tensor_scalar(out_deg[:], out_deg[:], 1.0, None, ALU.add).then_inc(deg_ready, 1)
            dve.wait_ge(deg_root_ready, 1)
            dve.reciprocal(inv_root[:], deg_root[:]).then_inc(gcn_adj_ready, 1)
            for i in range(1, HOPS + 1):
                for m in range(NT):
                    if i < HOPS:
                        dve.wait_ge(hi_ready, i * NT + m + 1)
                        dve.scalar_tensor_tensor(lo[i % 2][:, m, :], main[m][:], inv_row[:, m:m + 1],
                                                 hi[i % 2][:, m, :].bitcast(F32), ALU.mult, ALU.subtract).then_inc(lo_ready, 1)
                    else:
                        dve.wait_ge(hop_ready, (i - 1) * NT + m + 1)
                    dve.wait_ge(acc_ready, (i - 1) * NT + m + 1)
                    dve.scalar_tensor_tensor(h[:, m, :], main[m][:], dw_inv[:, i - 1, m:m + 1], h[:, m, :], ALU.mult, ALU.add)\
                        .then_inc(acc_ready, 1)
                    if i == HOPS:
                        dve.wait_ge(acc_ready, i * NT + m + 1)
                        link(dve.scalar_tensor_tensor(x[:, m, :], h[:, m, :], 0.0, x[:, m, :], ALU.max, ALU.add))
                        moments(1, m, x[:, m, :])
                        scale_and_shift(1, m)
            dve.wait_ge(wgt_deg_ready, 1)
            link(dve.tensor_scalar(wgt_deg[:], cnt_bank[:, 0:NT], 1.0, None, ALU.max))
            dve.reciprocal(inv_wgt[:], wgt_deg[:]).then_inc(wgt_deg_out, 1)
            for m in range(NT):
                dve.wait_ge(self_ready, m + 1)
                dve.wait_ge(self_biased, m + 1)
                dve.tensor_tensor(h[:, m, :], main[m][:], h[:, m, :], ALU.add).then_inc(self_out, 1)
            dve.wait_ge(rel_rows_loaded, 16 * R)
            for r in range(R):
                for m in range(NT):
                    dve.wait_ge(msg_ready, r * NT + m + 1)
                    dve.tensor_tensor(msg[r][:, m, :], main[m][:], brel[r], ALU.add).then_inc(msg_out, 1)
            dve.wait_ge(wgt_deg_out, 1)
            for m in range(NT):
                dve.wait_ge(agg_ready, m + 1)
                dve.wait_ge(self_out, m + 1)
                dve.scalar_tensor_tensor(h[:, m, :], main[m][:], inv_wgt[:, m:m + 1], h[:, m, :], ALU.mult, ALU.add)\
                    .then_inc(agg_out, 1)
                dve.wait_ge(agg_out, m + 1)
                moments(2, m, h[:, m, :])
                affine_norm(2, m, h[:, m, :], g1, be1, h[:, m, :]).then_inc(h_ready[2], 1)
            for m in range(NT):
                dve.wait_ge(down_ready, m + 1)
                dve.wait_ge(ffn_biased, m + 1)
                dve.tensor_tensor(h[:, m, :], main[m][:], h[:, m, :], ALU.add).then_inc(down_out, 1)
                dve.wait_ge(down_out, m + 1)
                moments(3, m, h[:, m, :])
                dve.wait_ge(ln2_biased, m + 1)
                link(affine_norm(3, m, h[:, m, :], g2, x[:, m, :], x[:, m, :]))
                moments(4, m, x[:, m, :])
                scale_and_shift(4, m)
            for t in range(NT):
                dve.wait_ge(cnt_t_ready, NT + t + 1)
                half = misc_bank if t % 2 else cnt_bank
                dve.scalar_tensor_tensor(adj[:, t, :], half[:], 0.0, eye_of(t), ALU.is_gt, ALU.add).then_inc(cnt_t_out, 1)
            for m in range(NT):
                dve.wait_ge(sup_hi, m + 1)
                dve.scalar_tensor_tensor(lo[0][:, m, :], main[m][:], inv_root[:, m:m + 1], hi[0][:, m, :].bitcast(F32),
                                         ALU.mult, ALU.subtract).then_inc(sup_out, 1)
            for m in range(NT):
                dve.wait_ge(gcn_ready, m + 1)
                dve.wait_ge(gcn_biased, m + 1)
                dve.scalar_tensor_tensor(x[:, m, :], main[m][:], inv_root[:, m:m + 1], x[:, m, :], ALU.mult, ALU.add)\
                    .then_inc(gcn_out, 1)
                dve.wait_ge(gcn_out, m + 1)
                moments(5, m, x[:, m, :])
                scale_and_shift(5, m)
            dve.wait_ge(cnt_ready, 1)
            link(dve.tensor_scalar(inv_cnt[:], cnt_bank[:], 1.0, None, ALU.max))
            link(dve.reciprocal(inv_cnt[:], inv_cnt[:]))
            for layer in range(2):
                for k in range(KT):
                    dve.wait_ge(mean_ready[layer], k + 1)
                    dve.tensor_tensor(agg_t[layer][:, k, :], main[k][:], inv_cnt[:], ALU.mult).then_inc(mean_out[layer], 1)
                for m in range(NT):
                    dve.wait_ge(sage_ready[layer], m + 1)
                    if layer == 0:
                        dve.wait_ge(late_rows_loaded, 16 * 3)
                        dve.tensor_tensor(h[:, m, :], main[m][:], bl1, ALU.add).then_inc(sage_out[0], 1)
                    else:
                        dve.wait_ge(sage_biased, m + 1)
                        dve.tensor_tensor(x[:, m, :], main[m][:], x[:, m, :], ALU.add).then_inc(sage_out[1], 1)

        @block.tensor
        def _(pe):
            def fill(use, blocks):
                if use >= 2:
                    pe.wait_ge(t_out, use - 1)
                for i, b in enumerate(blocks):
                    ins = pe.transpose(t_bank[use % 2][:, i * P:(i + 1) * P], b, ident[:])
                ins.then_inc(t_ready, 1)

            def fill_h(what, t, ready):
                pe.wait_ge(ready, t + 1)
                fill(use_of(what, t), [h[:, t, k * P:(k + 1) * P] for k in range(KT)])

            def fill_sage(what, q, k):
                pe.wait_ge(sage_loaded[q], 16)
                fill(use_of(what, k), [sage_raw[q][:, o, k * P:(k + 1) * P] for o in range(KT)])

            def product(bank, pairs):
                for i, (left, right) in enumerate(pairs):
                    ins = pe.matmul(bank[:], left, right, start=(i == 0), stop=(i == len(pairs) - 1))
                return ins

            def rows_by(weight, m):
                return [(h_t[:, k, m * P:(m + 1) * P], weight[:, k, :]) for k in range(KT)]

            def transpose_then(what, ready, each):
                fill_h(what, 0, ready)
                for t in range(NT):
                    if t + 1 < NT:
                        fill_h(what, t + 1, ready)
                    pe.wait_ge(t_out, use_of(what, t) + 1)
                    each(t)

            def transpose_counts(base):
                for t in range(NT):
                    n = base + t
                    if t >= 2:
                        pe.wait_ge(cnt_t_out, n - 1)
                    bank = misc_bank if t % 2 else cnt_bank
                    for s in range(NT):
                        ins = pe.transpose(bank[:, s * P:(s + 1) * P], count[s][:, t * P:(t + 1) * P], ident[:])
                    ins.then_inc(cnt_t_ready, 1)

            transpose_counts(0)
            pe.wait_ge(w0_loaded, 16)

            def project(m):
                product(main[m], rows_by(w0, m)).then_inc(proj_ready, 1)

            transpose_then(H0, h_ready[0], project)
            for i in range(1, HOPS + 1):
                src = (i - 1) % 2
                pe.wait_ge(cnt_t_out, NT)
                pe.wait_ge(lo_ready, i * NT)
                pe.wait_ge(acc_ready, i * NT)
                for m in range(NT):
                    cols = slice(m * P, (m + 1) * P)
                    pairs = [(adj[:, s, cols], part[src][:, s, :]) for part in (hi, lo) for s in range(NT)]
                    product(main[m], pairs).then_inc(hop_ready, 1)
            pe.wait_ge(wgt_add, R - 1)
            for m in range(NT):
                for s in range(NT):
                    ins = pe.matmul(cnt_bank[:, m:m + 1], wgt_sum[:, s, m * P:(m + 1) * P], ones[:, 0:1],
                                    start=(s == 0), stop=(s == NT - 1))
            ins.then_inc(wgt_deg_ready, 1)
            pe.wait_ge(wself_loaded, 16)

            def by_self(m):
                pe.wait_ge(acc_ready, HOPS * NT + m + 1)
                product(main[m], rows_by(wself, m)).then_inc(self_ready, 1)

            transpose_then(H1, h_ready[1], by_self)
            for r in range(R):
                pe.wait_ge(wrel_loaded[r], 16)
                for m in range(NT):
                    if r == 0:
                        pe.wait_ge(self_out, m + 1)
                    else:
                        pe.wait_ge(msg_out, (r - 1) * NT + m + 1)
                    product(main[m], rows_by(wrel[r], m)).then_inc(msg_ready, 1)
            pe.wait_ge(msg_out, R * NT)
            for m in range(NT):
                cols = slice(m * P, (m + 1) * P)
                pairs = [(wall[:, s, r, cols], msg[r][:, s, :]) for r in range(R) for s in range(NT)]
                product(main[m], pairs).then_inc(agg_ready, 1)
            for t in range(NT):
                fill_h(H2, t, h_ready[2])
            pe.wait_ge(t_out, use_of(H2, NT - 1) + 1)
            pe.wait_ge(wf1_loaded, 16)
            for g in range(GT):
                if g < 4:
                    pe.wait_ge(agg_out, g + 1)
                else:
                    pe.wait_ge(up_out, g - 3)
                pairs = [(wf1[:, k, g * P:(g + 1) * P], h_t[:, k, :]) for k in range(KT)]
                product(main[g % 4], pairs).then_inc(up_ready, 1)
            pe.wait_ge(up_out, GT)
            pe.wait_ge(wf2_loaded, 16)
            for m in range(NT):
                pairs = [(hid[:, g, m * P:(m + 1) * P], wf2[:, g, :]) for g in range(GT)]
                product(main[m], pairs).then_inc(down_ready, 1)
                fill_sage(WL1, 0, m)
            pe.wait_ge(wgt_deg_out, 1)
            transpose_counts(NT)
            pe.wait_ge(w2_loaded, 16)
            for t in range(NT):
                fill_h(H3, t, h_ready[4])
            for m in range(NT):
                pe.wait_ge(t_out, use_of(H3, m) + 1)
                pe.wait_ge(down_out, m + 1)
                product(main[m], rows_by(w2, m)).then_inc(sup_ready, 1)
                fill_sage(WR1, 1, m)
            pe.wait_ge(cnt_t_out, 2 * NT)
            pe.wait_ge(sup_out, NT)
            for m in range(NT):
                cols = slice(m * P, (m + 1) * P)
                pairs = [(adj[:, s, cols], part[0][:, s, :]) for part in (hi, lo) for s in range(NT)]
                product(main[m], pairs).then_inc(gcn_ready, 1)
                fill_sage(WL2, 2, m)
            product(cnt_bank, [(ones[:], count[s]) for s in range(NT)]).then_inc(cnt_ready, 1)
            for layer in range(2):
                if layer == 0:
                    for t in range(NT):
                        fill_h(H4, t, h_ready[5])
                    pe.wait_ge(gcn_out, NT)
                else:
                    for t in range(NT):
                        fill_h(H5, t, relu_ready)
                for k in range(KT):
                    pairs = [(h[:, s, k * P:(k + 1) * P], count[s]) for s in range(NT)]
                    product(main[k], pairs).then_inc(mean_ready[layer], 1)
                    if layer == 0:
                        fill_sage(WR2, 3, k)
                pe.wait_ge(mean_out[layer], KT)
                wl, wr = 2 * layer, 2 * layer + 1
                what = H5 if layer else H4
                pe.wait_ge(t_out, use_of(what if layer else WR2, NT - 1) + 1)
                for m in range(NT):
                    cols = slice(m * P, (m + 1) * P)
                    pairs = [(agg_t[layer][:, k, cols], sage(wl, k)) for k in range(KT)]
                    pairs += [(h_t[:, k, cols], sage(wr, k)) for k in range(KT)]
                    product(main[m], pairs).then_inc(sage_ready[layer], 1)


_INS = ['x', 'src', 'dst', 'edge_type_4', 'edge_weight', 'L0_gnn_W', 'L0_gnn_b', 'L0_gnn_diffusion_weights',
        'L1_gnn_W_self', 'L1_gnn_b_self', 'L1_gnn_W_rel', 'L1_gnn_b_rel', 'L1_gnn_ln1_g', 'L1_gnn_ln1_b', 'L1_gnn_ln2_g',
        'L1_gnn_ln2_b', 'L1_gnn_W_ffn1', 'L1_gnn_b_ffn1', 'L1_gnn_W_ffn2', 'L1_gnn_b_ffn2', 'L2_gnn_weight', 'L2_gnn_bias',
        'L3_gnn_Wl1', 'L3_gnn_bl1', 'L3_gnn_Wr1', 'L3_gnn_Wl2', 'L3_gnn_bl2', 'L3_gnn_Wr2']


def kernel(**inputs):
    import numpy as _np
    import concourse.bacc as _bacc
    from concourse import mybir as _mybir
    from concourse.bass_utils import run_bass_kernel_spmd as _run

    nc = _bacc.Bacc("TRN2", target_bir_lowering=False, num_devices=1)
    arrays, args = {}, []
    for name in _INS:
        a = _np.ascontiguousarray(inputs[name])
        arrays[f"in_{name}"] = a
        args.append(nc.dram_tensor(f"in_{name}", a.shape, _mybir.dt.from_np(a.dtype), kind="ExternalInput").ap())
    args.append(nc.dram_tensor("out", (N, D), F32, kind="ExternalOutput").ap())
    gnn_program(nc, *args)
    r = _run(nc, [arrays], core_ids=[0])
    return r.results[0]["out"]
```

```python
from contextlib import ExitStack

import concourse.bass as bass
from concourse import mybir

F32 = mybir.dt.float32
F32R = mybir.dt.float32r
BF16 = mybir.dt.bfloat16
F16 = mybir.dt.float16
I32 = mybir.dt.int32
ALU = mybir.AluOpType
ACT = mybir.ActivationFunctionType
AX = mybir.AxisListType
PE, DVE = mybir.EngineType.PE, mybir.EngineType.DVE

P = 128
N = 512
D = 512
E = 16384
R = 4
NT = N // P
KT = D // P
CH = E // P
WD = 8
NW = N // WD
WC = 4
V = 4
WK = R * WD
OUT_R = R + 1
GROUP = 4
UNROLL = 2 * GROUP
RING = UNROLL
HOT_WIN = CH // WC
F1 = 2 * D
GT = F1 // P
EPS = 1e-5
HOPS = 3
assert N == D and V * WK == P and HOT_WIN % UNROLL == 0 and NW > HOT_WIN and E % P == 0


def gnn_program(nc, x_in, src_in, dst_in, typ_in, wgt_in, w0_in, b0_in, dw_in, wself_in, bself_in, wrel_in, brel_in,
                g1_in, be1_in, g2_in, be2_in, wf1_in, bf1_in, wf2_in, bf2_in, w2_in, b2_in,
                wl1_in, bl1_in, wr1_in, wl2_in, bl2_in, wr2_in, out):
    with ExitStack() as keep:
        def sem(name):
            return keep.enter_context(nc.semaphore(name))

        def sb(name, shape, dt):
            return keep.enter_context(nc.sbuf_tensor(name, shape, dt))

        wall = sb("wall", [P, NT, OUT_R, N], F32)
        x = sb("x", [P, NT, D], F32)
        ident = sb("ident", [P, P], F32)
        ones = sb("ones", [P, P], F32)
        psum = [keep.enter_context(nc.psum_tensor(f"bank{i}", [P, 512], F32)) for i in range(8)]
        eps = sb("eps", [P, 1], F32)
        build_matrices(nc, sem, wall, x, ident, ones, eps, psum, x_in, src_in, dst_in, typ_in, wgt_in, w0_in, b0_in)
        run_blocks(nc, sem, wall, x, ident, ones, eps, psum, x_in, dw_in, wself_in, bself_in, wrel_in, brel_in,
                   g1_in, be1_in, g2_in, be2_in, wf1_in, bf1_in, wf2_in, bf2_in, w2_in, b2_in,
                   wl1_in, bl1_in, wr1_in, wl2_in, bl2_in, wr2_in, out)


def build_matrices(nc, sem, wall, x, ident, ones, eps, psum, x_in, src_in, dst_in, typ_in, wgt_in, w0_in, b0_in):
    with ExitStack() as ctx:
        def sb(name, shape, dt):
            return ctx.enter_context(nc.sbuf_tensor(name, shape, dt))

        src_hot = sb("src_hot", [P, CH, N], BF16)
        win = sb("win", [P, RING, WC, V, WK], BF16)
        z_sb = sb("z_sb", [P, GROUP, N], F32)
        key_iota = sb("key_iota", [P, R, N], F16)
        key_t = sb("key_t", [P, CH], F32)
        src_t = sb("src_t", [P, CH], F32)
        parts = sb("parts", [P, CH, V - 1], F32)
        fold = sb("fold", [P, OUT_R, WD], F32)
        win_lo = sb("win_lo", [P, NW], F32)
        next_dst_i = sb("next_dst_i", [P, 1], I32)
        next_dst = sb("next_dst", [P, 1], F32)
        viol = sb("viol", [P, 4], F32)
        first_chunk = sb("first_chunk", [P, NW], I32)
        slow_flag = sb("slow_flag", [P, 1], I32)
        stats = sb("stats0", [P, NT, 6], F32)
        mean_var = sb("mean_var0", [P, NT, 2], F32)
        std = sb("std0", [P, NT], F32)
        rstd = sb("rstd0", [P, NT], F32)
        shift = sb("shift0", [P, NT], F32)

        room = [wall[:, t, :, :].rearrange("p r n -> p (r n)") for t in range(NT)]
        key_iota_i = room[0][:, 0:R * N].bitcast(I32)
        h_t = room[0][:, 0:KT * N].rearrange("p (k n) -> p k n", k=KT)
        w0 = room[2][:, 0:KT * D].rearrange("p (k n) -> p k n", k=KT)
        h = room[3][:, 0:NT * D].rearrange("p (t n) -> p t n", t=NT)
        taken = [0]

        def small(*shape):
            size = 1
            for n in shape:
                size *= n
            ap = room[1][:, taken[0]:taken[0] + size]
            taken[0] += size
            return ap.rearrange("p (a b) -> p a b", a=shape[0]) if len(shape) == 2 else ap

        e_int = small(3, P).bitcast(I32)
        e_wgt = small(P)
        e_f32 = small(3, P)
        wgt_t = small(CH)
        rest = small(2, CH)
        part_b = small(V - 1, CH // 2).bitcast(BF16)
        chunk_cmp = small(2, NW)
        disorder = small(P)
        span = small(3, NW)
        b0 = small(D)
        slow_src, slow_key, zeros = src_hot[:, 0, :], src_hot[:, 1:1 + V, :], src_hot[:, 1 + V, :]

        dst_loaded, src_loaded, typ_loaded, wgt_loaded = (sem(f"{n}_loaded") for n in ("dst", "src", "typ", "wgt"))
        x_loaded, w0_loaded, b0_loaded = sem("x_loaded"), sem("w0_loaded"), sem("b0_loaded")
        next_set, next_loaded = sem("next_set"), sem("next_loaded")
        const_set, const_ready = sem("const_set"), sem("const_ready")
        iota_ready = sem("iota_ready")
        edges_ready, edges_t_ready = sem("edges_ready"), sem("edges_t_ready")
        cmp_ready, cmp_sum_ready, plan_ready = sem("cmp_ready"), sem("cmp_sum_ready"), sem("plan_ready")
        chain_sem = sem("build_chain")
        var_ready, std_ready, shift_ready, h_ready = sem("var0_ready"), sem("std0_ready"), sem("shift0_ready"), sem("h0_ready")
        t_ready, t_out, proj_ready, proj_out = sem("h0_t_ready"), sem("h0_t_out"), sem("proj_ready"), sem("proj_out")
        hot_ready, win_hot, win_ready = sem("hot_ready"), sem("win_hot"), sem("win_ready")
        z_ready, z_copied, folded, side_free = sem("z_ready"), sem("z_copied"), sem("folded"), sem("side_free")
        slow_free, slow_ready, slow_sum, slow_out = sem("slow_free"), sem("slow_ready"), sem("slow_sum"), sem("slow_out")
        slow_cnt, slow_cnt_out, slow_zero = sem("slow_cnt"), sem("slow_cnt_out"), sem("slow_zero")

        z_bank = proj_bank = psum[0:4]
        out_bank = [psum[4:6], psum[6:8]]
        t_bank, edge_bank, cmp_bank = psum[4:6], psum[6], psum[7]
        chunked = "(c e) -> c e"

        def load_flag(engine, kind):
            return engine.to_reg(nc.values_load_multi_w_load_instructions(
                slow_flag[0:1, 0:1], [kind], min_val=0, max_val=1,
                skip_runtime_bounds_check_because="the chip writes 0 or 1")[1][0])

        def load_starts(kind, i):
            return nc.values_load_multi_w_load_instructions(
                first_chunk[0:1, bass.ds(i * UNROLL, UNROLL)], [kind], min_val=0, max_val=CH - WC,
                skip_runtime_bounds_check_because="clamped to that on the chip")[1]

        block = ctx.enter_context(nc.Block())

        @block.sync
        def _(sp):
            sp.dma_start(e_int[:, 0, :], dst_in.rearrange(chunked, e=P)).then_inc(dst_loaded, 16)
            sp.wait_ge(next_set, 1)
            sp.dma_start(next_dst_i[0:CH - 1, :], dst_in.rearrange(chunked, e=P)[1:CH, 0:1],
                         allow_slow_non_contiguous=True).then_inc(next_loaded, 16)
            sp.dma_start(x[:], x_in.rearrange("(t p) f -> p t f", p=P)).then_inc(x_loaded, 16)
            sp.dma_start(w0, w0_in.rearrange("(k p) n -> p k n", p=P)).then_inc(w0_loaded, 16)

        @block.gpsimd
        def _(pool):
            pool.memset(next_dst_i[:], N).then_inc(next_set, 1)
            pool.memset(ident[:], 0.0).then_inc(const_set, 1)
            pool.memset(fold[:], 0.0).then_inc(const_set, 1)
            pool.memset(ones[:], 1.0).then_inc(const_ready, 1)
            pool.memset(eps[:], EPS).then_inc(const_ready, 1)
            pool.iota(win_lo[:], pattern=[[WD, NW]], base=0, channel_multiplier=0,
                      allow_small_or_imprecise_dtypes=True).then_inc(const_ready, 1)
            pool.wait_ge(const_set, 2)
            pool.affine_select(out=ident[:], in_=ident[:], compare_op=ALU.not_equal, fill=1.0, base=0,
                               pattern=[[-1, P]], channel_multiplier=1).then_inc(const_ready, 1)
            pool.iota(key_iota_i, pattern=[[1, R * N]], base=0, channel_multiplier=0).then_inc(iota_ready, 1)
            pool.wait_ge(iota_ready, 1)
            pool.tensor_copy(key_iota[:].rearrange("p r n -> p (r n)"), key_iota_i).then_inc(iota_ready, 1)
            for v in range(V - 1):
                last = pool.affine_select(out=fold[:, 0:R, :], in_=fold[:, 0:R, :], compare_op=ALU.not_equal, fill=1.0,
                                          base=-WK * v, pattern=[[-WD, R], [-1, WD]], channel_multiplier=1)
                last.then_inc(const_set, 1)
                pool.wait_ge(const_set, 3 + v)
            for r in range(R):
                last = pool.affine_select(out=fold[:, R, :], in_=fold[:, R, :], compare_op=ALU.not_equal, fill=1.0,
                                          base=-WK * (V - 1) - WD * r, pattern=[[-1, WD]], channel_multiplier=1)
                last.then_inc(const_set, 1)
                pool.wait_ge(const_set, 2 + V + r)
            pool.dma_start(b0, b0_in.partition_broadcast(P)).then_inc(b0_loaded, 16)

        @block.scalar
        def _(act):
            act.dma_start(e_int[:, 1, :], src_in.rearrange(chunked, e=P)).then_inc(src_loaded, 16)
            act.dma_start(e_int[:, 2, :], typ_in.rearrange(chunked, e=P)).then_inc(typ_loaded, 16)
            act.dma_start(e_wgt, wgt_in.rearrange(chunked, e=P)).then_inc(wgt_loaded, 16)
            act.wait_ge(const_ready, 4)
            for t in range(NT):
                act.wait_ge(var_ready, t + 1)
                act.activation(std[:, t:t + 1], mean_var[:, t, 1:2], ACT.Sqrt, bias=eps[:]).then_inc(std_ready, 1)
            for t in range(NT):
                act.wait_ge(shift_ready, t + 1)
                act.activation(h[:, t, :], x[:, t, :], ACT.Relu, bias=shift[:, t:t + 1], scale=rstd[:, t:t + 1])\
                    .then_inc(h_ready, 1)
            act.wait_ge(iota_ready, 2)
            for t in range(NT):
                act.wait_ge(t_ready, t + 1)
                act.activation(h_t[:, :, t * P:(t + 1) * P], t_bank[t % 2][:].rearrange("p (k n) -> p k n", k=KT),
                               ACT.Copy).then_inc(t_out, 1)
            act.wait_ge(plan_ready, 2)
            slow = load_flag(act, mybir.EngineType.Activation)

            def copy_group(first, i, side):
                for k in range(GROUP):
                    j = side * GROUP + k
                    act.wait_ge(z_ready, i * UNROLL + j + 1)
                    if not (first and side == 0):
                        act.wait_ge(folded, i * UNROLL + j - GROUP + 1)
                    act.activation(z_sb[:, k, :], z_bank[k][:], ACT.Copy).then_inc(z_copied, 1)
                if not (first and side == 0):
                    copy_out(i * UNROLL + (side - 1) * GROUP, 1 - side)

            def copy_out(w0, side):
                act.wait_ge(folded, w0 + GROUP)
                for half in range(2):
                    got = out_bank[side][half][:, 0:2 * OUT_R * GROUP * WD].rearrange("p (t r d) -> p t r d", t=2, r=OUT_R)
                    act.activation(wall[:, 2 * half:2 * half + 2, :, bass.ds(w0 * WD, GROUP * WD)], got, ACT.Copy)\
                        .then_inc(side_free, 1)

            with act.If_eq(slow, 0):
                for side in range(2):
                    copy_group(True, 0, side)
                with act.Fori(1, NW // UNROLL) as i:
                    for side in range(2):
                        copy_group(False, i, side)
                copy_out(NW - GROUP, 1)

        @block.vector
        def _(dve):
            links = [0]

            def link(ins):
                links[0] += 1
                ins.then_inc(chain_sem, 1)
                dve.wait_ge(chain_sem, links[0])

            dve.wait_ge(dst_loaded, 16)
            dve.tensor_copy(e_f32[:, 0, :], e_int[:, 0, :]).then_inc(edges_ready, 1)
            dve.wait_ge(src_loaded, 16)
            dve.tensor_copy(e_f32[:, 1, :], e_int[:, 1, :]).then_inc(edges_ready, 1)
            dve.wait_ge(typ_loaded, 16)
            dve.scalar_tensor_tensor(e_f32[:, 2, :], e_int[:, 2, :], float(N), e_int[:, 0, :], ALU.mult, ALU.add)\
                .then_inc(edges_ready, 1)
            dve.wait_ge(edges_ready, 1)
            dve.wait_ge(const_ready, 3)
            dve.tensor_scalar(chunk_cmp[:, 0, :], win_lo[:], e_f32[:, 0, P - 1:P], None, ALU.is_gt).then_inc(cmp_ready, 1)
            link(dve.tensor_scalar(span[:, 0, :], win_lo[:], float(WD), None, ALU.add))
            dve.tensor_scalar(chunk_cmp[:, 1, :], span[:, 0, :], e_f32[:, 0, 0:1], None, ALU.is_gt).then_inc(cmp_ready, 1)
            dve.wait_ge(next_loaded, 16)
            link(dve.tensor_copy(next_dst[:], next_dst_i[:]))
            dve.tensor_tensor(viol[:, 1:2], e_f32[:, 0, P - 1:P], next_dst[:], ALU.is_gt).then_inc(cmp_ready, 1)
            link(dve.tensor_tensor(disorder[:, 0:P - 1], e_f32[:, 0, 0:P - 1], e_f32[:, 0, 1:P], ALU.is_gt))
            dve.tensor_reduce(viol[:, 0:1], disorder[:, 0:P - 1], AX.X, ALU.add).then_inc(cmp_ready, 1)

            dve.wait_ge(x_loaded, 16)
            for t in range(NT):
                link(dve.bn_stats(stats[:, t, :], x[:, t, :]))
                dve.bn_aggr(mean_var[:, t, :], stats[:, t, :]).then_inc(var_ready, 1)
            dve.wait_ge(std_ready, NT)
            link(dve.reciprocal(rstd[:], std[:]))
            for t in range(NT):
                dve.tensor_scalar(shift[:, t:t + 1], mean_var[:, t, 0:1], rstd[:, t:t + 1], -1.0, ALU.mult, ALU.mult)\
                    .then_inc(shift_ready, 1)

            dve.wait_ge(edges_t_ready, 3)
            dve.tensor_copy(src_t[:], edge_bank[:, 0:P]).then_inc(edges_ready, 1)
            dve.tensor_copy(key_t[:], edge_bank[:, P:2 * P]).then_inc(edges_ready, 1)
            link(dve.tensor_copy(wgt_t, edge_bank[:, 2 * P:3 * P]))
            link(dve.tensor_copy(part_b[:, 0, :], wgt_t))
            link(dve.tensor_tensor(rest[:, 0, :], wgt_t, part_b[:, 0, :], ALU.subtract))
            link(dve.tensor_copy(part_b[:, 1, :], rest[:, 0, :]))
            link(dve.tensor_tensor(rest[:, 1, :], rest[:, 0, :], part_b[:, 1, :], ALU.subtract))
            link(dve.tensor_copy(part_b[:, 2, :], rest[:, 1, :]))
            link(dve.tensor_copy(parts[:].rearrange("p c v -> p v c"), part_b))

            dve.wait_ge(cmp_sum_ready, 1)
            link(dve.tensor_scalar(span[:, 0, :], cmp_bank[:, 0:NW], float(CH - WC), None, ALU.min))
            dve.tensor_copy(first_chunk[:], span[:, 0, :]).then_inc(plan_ready, 1)
            link(dve.tensor_tensor(span[:, 1, :], cmp_bank[:, NW:2 * NW], span[:, 0, :], ALU.subtract))
            link(dve.tensor_scalar(span[:, 2, :], span[:, 1, :], float(WC), None, ALU.is_gt))
            link(dve.tensor_reduce(viol[:, 2:3], span[:, 2, :], AX.X, ALU.add))
            dve.tensor_copy(viol[:, 3:4], cmp_bank[:, 2 * NW:2 * NW + 1]).then_inc(side_free, 1)
            dve.wait_ge(side_free, 1)
            link(dve.tensor_tensor(span[:, 1, 0:1], viol[:, 2:3], viol[:, 3:4], ALU.add))
            dve.tensor_scalar(slow_flag[:], span[:, 1, 0:1], 0.0, None, ALU.is_gt).then_inc(plan_ready, 1)
            dve.wait_ge(plan_ready, 2)
            slow = load_flag(dve, DVE)
            dve.wait_ge(iota_ready, 2)
            dve.wait_ge(edges_ready, 5)

            def windows(first, i, side, starts, with_hots):
                mine = range(side * GROUP, (side + 1) * GROUP)
                for j in mine:
                    if with_hots:
                        for c in range(WC):
                            n = (i * UNROLL + j) * WC + c
                            dve.tensor_scalar(src_hot[:, bass.ds(n, 1), :].squeeze(1), key_iota[:, 0, :],
                                              src_t[:, bass.ds(n, 1)], None, ALU.is_equal).then_inc(hot_ready, 1)
                    if not first:
                        dve.wait_ge(z_ready, i * UNROLL + j - RING + 1)
                    key = key_t[:, bass.ds(starts[j], WC)].unsqueeze(2).unsqueeze(3).broadcast_to([P, WC, R, WD])
                    want = key_iota[:, :, bass.ds((i * UNROLL + j) * WD, WD)].unsqueeze(1).broadcast_to([P, WC, R, WD])
                    dve.tensor_tensor(win[:, j, :, V - 1, :].rearrange("p c (r d) -> p c r d", r=R),
                                      key, want, ALU.is_equal).then_inc(win_hot, 1)
                for j in mine:
                    dve.wait_ge(win_hot, i * UNROLL + j + 1)
                    hot = win[:, j, :, V - 1, :].unsqueeze(2).broadcast_to([P, WC, V - 1, WK])
                    wgt = parts[:, bass.ds(starts[j], WC), :].unsqueeze(3).broadcast_to([P, WC, V - 1, WK])
                    dve.tensor_tensor(win[:, j, :, 0:V - 1, :], hot, wgt, ALU.mult).then_inc(win_ready, 1)

            def pass_of_windows(first, i, with_hots):
                starts = load_starts(DVE, i)
                for side in range(2):
                    windows(first, i, side, starts, with_hots)

            def projection():
                dve.wait_ge(b0_loaded, 16)
                dve.wait_ge(h_ready, NT)
                for m in range(NT):
                    dve.wait_ge(proj_ready, m + 1)
                    dve.tensor_tensor(x[:, m, :], proj_bank[m][:], b0, ALU.add).then_inc(proj_out, 1)

            with dve.If_eq(slow, 0):
                pass_of_windows(True, 0, True)
                projection()
                with dve.Fori(1, HOT_WIN // UNROLL) as i:
                    pass_of_windows(False, i, True)
                with dve.Fori(HOT_WIN // UNROLL, NW // UNROLL) as i:
                    pass_of_windows(False, i, False)

            with dve.If_ne(slow, 0):
                projection()
                dve.memset(zeros, 0.0).then_inc(slow_zero, 1)
                dve.memset(slow_src, 0.0).then_inc(slow_free, 1)
                with dve.Fori(0, R) as r:
                    with dve.Fori(0, CH) as c:
                        dve.wait_ge(slow_free, r * CH + c + 1)
                        dve.tensor_scalar(slow_src, key_iota[:, 0, :], src_t[:, bass.ds(c, 1)], None, ALU.is_equal)\
                            .then_inc(slow_ready, 1)
                        for v in range(V - 1):
                            dve.tensor_scalar(slow_key[:, v, :], key_iota[:, bass.ds(r, 1), :].squeeze(1),
                                              key_t[:, bass.ds(c, 1)], parts[:, bass.ds(c, 1), v], ALU.is_equal, ALU.mult)\
                                .then_inc(slow_ready, 1)
                        dve.tensor_scalar(slow_key[:, V - 1, :], key_iota[:, bass.ds(r, 1), :].squeeze(1),
                                          key_t[:, bass.ds(c, 1)], None, ALU.is_equal).then_inc(slow_ready, 1)
                    dve.wait_ge(slow_sum, r + 1)
                    for t in range(NT):
                        dve.tensor_copy(wall[:, t, bass.ds(r, 1), :].squeeze(1), psum[t][:]).then_inc(slow_out, 1)
                dve.wait_ge(slow_cnt, 1)
                for t in range(NT):
                    dve.tensor_copy(wall[:, t, R, :], psum[NT + t][:]).then_inc(slow_cnt_out, 1)

        @block.tensor
        def _(pe):
            pe.wait_ge(const_ready, 4)
            pe.wait_ge(edges_ready, 2)
            pe.transpose(edge_bank[:, 0:P], e_f32[:, 1, :], ident[:]).then_inc(edges_t_ready, 1)
            pe.wait_ge(edges_ready, 3)
            pe.transpose(edge_bank[:, P:2 * P], e_f32[:, 2, :], ident[:]).then_inc(edges_t_ready, 1)
            pe.wait_ge(wgt_loaded, 16)
            pe.transpose(edge_bank[:, 2 * P:3 * P], e_wgt, ident[:]).then_inc(edges_t_ready, 1)
            pe.wait_ge(cmp_ready, 4)
            pe.matmul(cmp_bank[:, 0:2 * NW], ones[:], chunk_cmp.rearrange("p a w -> p (a w)"), start=True, stop=True)
            pe.matmul(cmp_bank[:, 2 * NW:2 * NW + 1], ones[:], viol[:, 0:1], start=False, stop=False, skip_group_check=True)
            pe.matmul(cmp_bank[:, 2 * NW:2 * NW + 1], ones[:], viol[:, 1:2], start=False, stop=True, skip_group_check=True)\
                .then_inc(cmp_sum_ready, 1)
            for t in range(NT):
                pe.wait_ge(h_ready, t + 1)
                if t >= 2:
                    pe.wait_ge(t_out, t - 1)
                for k in range(KT):
                    ins = pe.transpose(t_bank[t % 2][:, k * P:(k + 1) * P], h[:, t, k * P:(k + 1) * P], ident[:])
                ins.then_inc(t_ready, 1)
            pe.wait_ge(w0_loaded, 16)
            for m in range(NT):
                pe.wait_ge(t_out, m + 1)
                for k in range(KT):
                    ins = pe.matmul(proj_bank[m][:], h_t[:, k, m * P:(m + 1) * P], w0[:, k, :],
                                    start=(k == 0), stop=(k == KT - 1))
                ins.then_inc(proj_ready, 1)
            pe.wait_ge(plan_ready, 2)
            slow = load_flag(pe, PE)

            def sum_group(first, i, side, starts, with_hots):
                for k in range(GROUP):
                    j = side * GROUP + k
                    pe.wait_ge(win_ready, i * UNROLL + j + 1)
                    if with_hots:
                        pe.wait_ge(hot_ready, (i * UNROLL + j + 1) * WC)
                    if first and side == 0:
                        pe.wait_ge(proj_out, k + 1)
                    else:
                        pe.wait_ge(z_copied, i * UNROLL + j - GROUP + 1)
                    for c in range(WC):
                        ins = pe.matmul(z_bank[k][:], win[:, j, c, :, :].rearrange("p v k -> p (v k)"),
                                        src_hot[:, bass.ds(starts[j] + c, 1), :].squeeze(1), start=(c == 0), stop=(c == WC - 1))
                    ins.then_inc(z_ready, 1)

            def fold_group(first, w0, side, freed):
                if not first:
                    pe.wait_ge(side_free, freed)
                for k in range(GROUP):
                    pe.wait_ge(z_copied, w0 + k + 1)
                    for t in range(NT):
                        col = (t % 2) * OUT_R * GROUP * WD
                        to = out_bank[side][t // 2][:, col:col + OUT_R * GROUP * WD]
                        to = to.rearrange("p (r w d) -> p r w d", r=OUT_R, w=GROUP)
                        ins = pe.matmul(to[:, :, k, :], z_sb[:, k, t * P:(t + 1) * P], fold[:], start=True, stop=True)
                    ins.then_inc(folded, 1)

            def pass_of_windows(first, i, with_hots):
                starts = load_starts(PE, i)
                for side in range(2):
                    sum_group(first, i, side, starts, with_hots)
                    if not (first and side == 0):
                        fold_group(first, i * UNROLL + (side - 1) * GROUP, 1 - side, 1 + (2 * i + side - 2) * 2)

            with pe.If_eq(slow, 0):
                pe.wait_ge(const_set, 2 + V - 1 + R)
                pass_of_windows(True, 0, True)
                with pe.Fori(1, HOT_WIN // UNROLL) as i:
                    pass_of_windows(False, i, True)
                with pe.Fori(HOT_WIN // UNROLL, NW // UNROLL) as i:
                    pass_of_windows(False, i, False)
                fold_group(False, NW - GROUP, 1, 1 + 2 * (NW // GROUP - 2))

            with pe.If_ne(slow, 0):
                pe.wait_ge(proj_out, NT)
                pe.wait_ge(slow_zero, 1)
                for t in range(NT):
                    pe.matmul(psum[NT + t][:], zeros[:, 0:P], zeros, start=True, stop=False)
                with pe.Fori(0, R) as r:
                    for t in range(NT):
                        pe.matmul(psum[t][:], zeros[:, 0:P], zeros, start=True, stop=False)
                    with pe.Fori(0, CH) as c:
                        pe.wait_ge(slow_ready, (r * CH + c + 1) * (V + 1))
                        for t in range(NT):
                            for v in range(V - 1):
                                pe.matmul(psum[t][:], slow_src[:, t * P:(t + 1) * P], slow_key[:, v, :], start=False, stop=False)
                            ins = pe.matmul(psum[NT + t][:], slow_src[:, t * P:(t + 1) * P], slow_key[:, V - 1, :],
                                            start=False, stop=False)
                        ins.then_inc(slow_free, 1)
                    for t in range(NT):
                        ins = pe.matmul(psum[t][:], zeros[:, 0:P], zeros, start=False, stop=True)
                    ins.then_inc(slow_sum, 1)
                    pe.wait_ge(slow_out, r * NT + NT)
                for t in range(NT):
                    ins = pe.matmul(psum[NT + t][:], zeros[:, 0:P], zeros, start=False, stop=True)
                ins.then_inc(slow_cnt, 1)


H1, H2, WL1, H3, WR1, WL2, H4, WR2, H5 = range(9)


def use_of(what, t):
    return NT * what + t


def run_blocks(nc, sem, wall, x, ident, ones, eps, psum, x_in, dw_in, wself_in, bself_in, wrel_in, brel_in,
               g1_in, be1_in, g2_in, be2_in, wf1_in, bf1_in, wf2_in, bf2_in, w2_in, b2_in,
               wl1_in, bl1_in, wr1_in, wl2_in, bl2_in, wr2_in, out):
    with ExitStack() as ctx:
        def sb(name, shape, dt):
            return ctx.enter_context(nc.sbuf_tensor(name, shape, dt))

        slots = sb("slots", [P, 8, KT * D], F32)

        def place(n, k=KT):
            return slots[:, n:n + k // KT, :].rearrange("p a (k n) -> p (a k) n", k=KT)

        wself, wrel = place(1), [place(2 + r) for r in range(R)]
        msg = [place(6), place(7), place(0), place(1)]
        wgt_sum = place(7)
        wf1 = slots[:, 2:4, :].rearrange("p a n -> p (a n)").rearrange("p (k n) -> p k n", k=KT)
        wf2 = place(4, GT)
        hid = place(6, GT)
        w2 = place(0)
        sage_raw = [place(1), place(2), place(3), place(4)]
        agg_t = [place(6), place(7)]

        def sage(q, k):
            return wall[:, k, q, :]

        count = [wall[:, t, R, :] for t in range(NT)]
        h = sb("h", [P, NT, D], F32)
        h_t = sb("h_t", [P, KT, N], F32)
        adj = sb("adj", [P, NT, N], F32R)
        hi = [sb(f"hi{i}", [P, NT, D], F32R) for i in range(2)]
        lo = [sb(f"lo{i}", [P, NT, D], F32R) for i in range(2)]
        cur = sb("cur", [P, 2, D], F32)
        eye = sb("eye", [P, 2 * N - P], F32)
        bias = sb("bias", [P, 6 + R, D], F32)
        bself, g1, be1, g2, be2, bf2 = (bias[:, i, :] for i in range(6))
        brel = [bias[:, 6 + r, :] for r in range(R)]
        b2, bl1, bl2 = (bias[:, 6 + i, :] for i in range(3))
        bf1 = sb("bf1", [P, GT], F32)
        dw = sb("dw", [P, HOPS + 1], F32)
        dw_inv = sb("dw_inv", [P, HOPS, NT], F32)
        stats = sb("stats", [P, NT, 6], F32)
        mean_var = sb("mean_var", [P, NT, 2], F32)
        std = sb("std", [P, NT], F32)
        rstd = sb("rstd", [P, NT], F32)
        shift = sb("shift", [P, NT], F32)
        row_sum = sb("row_sum", [P, NT], F32)
        inv_row = sb("inv_row", [P, NT], F32)
        out_deg = sb("out_deg", [P, NT], F32)
        deg_root = sb("deg_root", [P, NT], F32)
        inv_root = sb("inv_root", [P, NT], F32)
        wgt_deg = sb("wgt_deg", [P, NT], F32)
        inv_wgt = sb("inv_wgt", [P, NT], F32)
        inv_cnt = sb("inv_cnt", [P, N], F32)

        rows_loaded, rel_rows_loaded, late_rows_loaded = sem("rows_loaded"), sem("rel_rows_loaded"), sem("late_rows_loaded")
        dw_loaded, bf1_loaded = sem("dw_loaded"), sem("bf1_loaded")
        x_again_loaded, wself_loaded, w2_loaded = sem("x_again_loaded"), sem("wself_loaded"), sem("w2_loaded")
        wrel_loaded = [sem(f"wrel{r}_loaded") for r in range(R)]
        wf1_loaded, wf2_loaded = sem("wf1_loaded"), sem("wf2_loaded")
        sage_loaded = [sem(f"sage{q}_loaded") for q in range(4)]
        out_stored = sem("out_stored")
        eye_set, eye_ready = sem("eye_set"), sem("eye_ready")
        wgt_add, self_biased, ffn_biased, ln2_biased = sem("wgt_add"), sem("self_biased"), sem("ffn_biased"), sem("ln2_biased")
        gcn_biased, sage_biased = sem("gcn_biased"), sem("sage_biased")
        TO_REL, MID, OUT_FFN, TO_GCN, TO_SAGE = range(5)
        NORMS = 5
        var_ready = [sem(f"var_ready{n}") for n in range(NORMS)]
        std_ready = [sem(f"std_ready{n}") for n in range(NORMS)]
        shift_ready = [sem(f"shift_ready{n}") for n in range(NORMS)]
        h_ready = [sem(f"h_ready{n}") for n in range(NORMS)]
        t_ready, t_out = sem("t_ready"), sem("t_out")
        cnt_ready, cnt_t_ready, cnt_t_out = sem("cnt_ready"), sem("cnt_t_ready"), sem("cnt_t_out")
        inv_row_ready, deg_ready, deg_root_ready, wgt_deg_ready, wgt_deg_out = (
            sem("inv_row_ready"), sem("deg_ready"), sem("deg_root_ready"), sem("wgt_deg_ready"), sem("wgt_deg_out"))
        gcn_adj_ready = sem("gcn_adj_ready")
        hi_ready, lo_ready, acc_ready, hop_ready = sem("hi_ready"), sem("lo_ready"), sem("acc_ready"), sem("hop_ready")
        self_ready, self_out, msg_ready, msg_out, agg_ready, agg_out = (
            sem("self_ready"), sem("self_out"), sem("msg_ready"), sem("msg_out"), sem("agg_ready"), sem("agg_out"))
        up_ready, up_out, down_ready, down_out = sem("up_ready"), sem("up_out"), sem("down_ready"), sem("down_out")
        sup_ready, sup_out, sup_hi, gcn_ready, gcn_out = (
            sem("sup_ready"), sem("sup_out"), sem("sup_hi"), sem("gcn_ready"), sem("gcn_out"))
        mean_ready, mean_out = [sem(f"mean_ready{i}") for i in range(2)], [sem(f"mean_out{i}") for i in range(2)]
        sage_ready, sage_out = [sem(f"sage_ready{i}") for i in range(2)], [sem(f"sage_out{i}") for i in range(2)]
        relu_ready = sem("relu_ready")
        chain_sem = sem("run_chain")

        main, t_bank, cnt_bank, misc_bank = psum[0:4], psum[4:6], psum[6], psum[7]

        def row(ap):
            return ap.partition_broadcast(P)

        def tiled(ap, p=P):
            return ap.rearrange("(k p) n -> p k n", p=p)

        block = ctx.enter_context(nc.Block())

        @block.sync
        def _(sp):
            sp.dma_start(wself, tiled(wself_in)).then_inc(wself_loaded, 16)
            sp.wait_ge(lo_ready, NT)
            sp.wait_ge(acc_ready, NT)
            sp.dma_start(x[:], tiled(x_in)).then_inc(x_again_loaded, 16)
            for r in range(R):
                sp.dma_start(wrel[r], tiled(wrel_in[r])).then_inc(wrel_loaded[r], 16)
            sp.wait_ge(msg_ready, R * NT)
            sp.dma_start(wf1, tiled(wf1_in)).then_inc(wf1_loaded, 16)
            sp.dma_start(wf2, tiled(wf2_in)).then_inc(wf2_loaded, 16)
            sp.wait_ge(agg_ready, NT)
            sp.dma_start(sage_raw[0], tiled(wl1_in)).then_inc(sage_loaded[0], 16)
            sp.dma_start(w2, tiled(w2_in)).then_inc(w2_loaded, 16)
            sp.wait_ge(up_ready, GT)
            sp.dma_start(sage_raw[1], tiled(wr1_in)).then_inc(sage_loaded[1], 16)
            sp.dma_start(sage_raw[2], tiled(wl2_in)).then_inc(sage_loaded[2], 16)
            sp.wait_ge(down_ready, NT)
            sp.dma_start(sage_raw[3], tiled(wr2_in)).then_inc(sage_loaded[3], 16)
            for m in range(NT):
                sp.wait_ge(sage_out[1], m + 1)
                sp.dma_start(out[m * P:(m + 1) * P, :], x[:, m, :]).then_inc(out_stored, 16)
            sp.wait_ge(out_stored, 16 * NT)

        @block.gpsimd
        def _(pool):
            pool.dma_start(dw[:], row(dw_in)).then_inc(dw_loaded, 16)
            for to, of in ((bself, bself_in), (g1, g1_in), (be1, be1_in), (g2, g2_in), (be2, be2_in), (bf2, bf2_in)):
                pool.dma_start(to, row(of)).then_inc(rows_loaded, 16)
            for r in range(R):
                pool.dma_start(brel[r], row(brel_in[r])).then_inc(rel_rows_loaded, 16)
            pool.dma_start(bf1[:], bf1_in.rearrange("(g p) -> p g", p=P), allow_slow_non_contiguous=True).then_inc(bf1_loaded, 16)
            pool.memset(eye[:], 0.0).then_inc(eye_set, 1)
            pool.wait_ge(eye_set, 1)
            pool.affine_select(out=eye[:], in_=eye[:], compare_op=ALU.not_equal, fill=1.0, base=N - P,
                               pattern=[[-1, 2 * N - P]], channel_multiplier=1).then_inc(eye_ready, 1)
            pool.tensor_tensor(wgt_sum, wall[:, :, 0, :], wall[:, :, 1, :], ALU.add).then_inc(wgt_add, 1)
            for r in range(2, R):
                pool.wait_ge(wgt_add, r - 1)
                pool.tensor_tensor(wgt_sum, wgt_sum, wall[:, :, r, :], ALU.add).then_inc(wgt_add, 1)
            pool.wait_ge(rows_loaded, 16 * 6)
            for t in range(NT):
                pool.wait_ge(t_ready, use_of(H1, t) + 1)
                pool.tensor_tensor(h[:, t, :], h[:, t, :], bself, ALU.add).then_inc(self_biased, 1)
                pool.wait_ge(h_ready[TO_REL], t + 1)
                pool.tensor_tensor(x[:, t, :], x[:, t, :], be2, ALU.add).then_inc(ln2_biased, 1)
            pool.wait_ge(msg_out, R * NT)
            for to, of in ((b2, b2_in), (bl1, bl1_in), (bl2, bl2_in)):
                pool.dma_start(to, row(of)).then_inc(late_rows_loaded, 16)
            for t in range(NT):
                pool.wait_ge(t_ready, use_of(H2, t) + 1)
                pool.tensor_tensor(h[:, t, :], h[:, t, :], bf2, ALU.add).then_inc(ffn_biased, 1)
            pool.wait_ge(late_rows_loaded, 16 * 3)
            for t in range(NT):
                pool.wait_ge(h_ready[TO_GCN], t + 1)
                pool.tensor_tensor(x[:, t, :], x[:, t, :], b2, ALU.add).then_inc(gcn_biased, 1)
            for t in range(NT):
                pool.wait_ge(h_ready[TO_SAGE], t + 1)
                pool.tensor_tensor(x[:, t, :], x[:, t, :], bl2, ALU.add).then_inc(sage_biased, 1)

        @block.scalar
        def _(act):
            def root(n, t):
                act.wait_ge(var_ready[n], t + 1)
                act.activation(std[:, t:t + 1], mean_var[:, t, 1:2], ACT.Sqrt, bias=eps[:]).then_inc(std_ready[n], 1)

            def norm_relu(n, t):
                act.wait_ge(shift_ready[n], t + 1)
                act.activation(h[:, t, :], x[:, t, :], ACT.Relu, bias=shift[:, t:t + 1], scale=rstd[:, t:t + 1])\
                    .then_inc(h_ready[n], 1)

            def empty(use, to):
                act.wait_ge(t_ready, use + 1)
                act.activation(to, t_bank[use % 2][:].rearrange("p (a n) -> p a n", n=to.shape[-1]) if len(to.shape) == 3
                               else t_bank[use % 2][:], ACT.Copy).then_inc(t_out, 1)

            def empty_h(what, t):
                empty(use_of(what, t), h_t[:, :, t * P:(t + 1) * P])

            def empty_sage(what, q, k):
                empty(use_of(what, k), sage(q, k))

            def norm_and_transposes(n, what):
                for t in range(NT):
                    root(n, t)
                    norm_relu(n, t)
                    if t > 0:
                        empty_h(what, t - 1)
                empty_h(what, NT - 1)

            for m in range(NT):
                act.activation(hi[0][:, m, :], x[:, m, :], ACT.Copy).then_inc(hi_ready, 1)
            act.wait_ge(deg_ready, 1)
            act.activation(deg_root[:], out_deg[:], ACT.Sqrt).then_inc(deg_root_ready, 1)
            act.wait_ge(inv_row_ready, 1)
            for i in range(1, HOPS):
                for m in range(NT):
                    act.wait_ge(hop_ready, (i - 1) * NT + m + 1)
                    act.activation(hi[i % 2][:, m, :], main[m][:], ACT.Copy, scale=inv_row[:, m:m + 1]).then_inc(hi_ready, 1)
            norm_and_transposes(TO_REL, H1)
            for t in range(NT):
                root(MID, t)
                if t > 0:
                    empty_h(H2, t - 1)
            empty_h(H2, NT - 1)
            act.wait_ge(bf1_loaded, 16)
            for g in range(GT):
                act.wait_ge(up_ready, g + 1)
                act.activation(hid[:, g, :], main[g % 4][:], ACT.Gelu, bias=bf1[:, g:g + 1]).then_inc(up_out, 1)
            for t in range(NT):
                empty_sage(WL1, 0, t)
                root(OUT_FFN, t)
                root(TO_GCN, t)
                norm_relu(TO_GCN, t)
            for t in range(NT):
                empty_h(H3, t)
            for m in range(NT):
                act.wait_ge(sup_ready, m + 1)
                act.activation(hi[0][:, m, :], main[m][:], ACT.Copy, scale=inv_root[:, m:m + 1]).then_inc(sup_hi, 1)
                empty_sage(WR1, 1, m)
            for t in range(NT):
                empty_sage(WL2, 2, t)
                root(TO_SAGE, t)
                norm_relu(TO_SAGE, t)
            for t in range(NT):
                empty_h(H4, t)
            for k in range(KT):
                empty_sage(WR2, 3, k)
            for t in range(NT):
                act.wait_ge(sage_out[0], t + 1)
                act.activation(h[:, t, :], h[:, t, :], ACT.Relu).then_inc(relu_ready, 1)
                if t > 0:
                    empty_h(H5, t - 1)
            empty_h(H5, NT - 1)

        @block.vector
        def _(dve):
            links = [0]

            def link(ins):
                links[0] += 1
                ins.then_inc(chain_sem, 1)
                dve.wait_ge(chain_sem, links[0])

            def moments(n, t, rows):
                link(dve.bn_stats(stats[:, t, :], rows))
                dve.bn_aggr(mean_var[:, t, :], stats[:, t, :]).then_inc(var_ready[n], 1)

            def inverse_std(n, t):
                dve.wait_ge(std_ready[n], t + 1)
                link(dve.reciprocal(rstd[:, t:t + 1], std[:, t:t + 1]))

            def scale_and_shift(n, t):
                inverse_std(n, t)
                dve.tensor_scalar(shift[:, t:t + 1], mean_var[:, t, 0:1], rstd[:, t:t + 1], -1.0, ALU.mult, ALU.mult)\
                    .then_inc(shift_ready[n], 1)

            def affine_norm(n, t, rows, gain, plus, to):
                inverse_std(n, t)
                link(dve.scalar_tensor_tensor(rows, rows, mean_var[:, t, 0:1], gain, ALU.subtract, ALU.mult))
                return dve.scalar_tensor_tensor(to, rows, rstd[:, t:t + 1], plus, ALU.mult, ALU.add)

            def eye_of(t):
                return eye[:, N - P - t * P:2 * N - P - t * P]

            dve.wait_ge(eye_ready, 1)
            for t in range(NT):
                dve.wait_ge(cnt_t_ready, t + 1)
                half = misc_bank if t % 2 else cnt_bank
                link(dve.tensor_tensor(cur[:, t % 2, :], half[:], count[t], ALU.add))
                dve.scalar_tensor_tensor(adj[:, t, :], cur[:, t % 2, :], 0.0, eye_of(t), ALU.is_gt, ALU.add,
                                         accum_out=row_sum[:, t:t + 1]).then_inc(cnt_t_out, 1)
            dve.wait_ge(cnt_t_out, NT)
            link(dve.tensor_scalar(inv_row[:], row_sum[:], 1.0, None, ALU.max))
            dve.reciprocal(inv_row[:], inv_row[:]).then_inc(inv_row_ready, 1)
            dve.wait_ge(dw_loaded, 16)
            dve.wait_ge(inv_row_ready, 1)
            for i in range(HOPS):
                link(dve.tensor_scalar(dw_inv[:, i, :], inv_row[:], dw[:, i + 1:i + 2], None, ALU.mult))
            for m in range(NT):
                dve.tensor_scalar(h[:, m, :], x[:, m, :], dw[:, 0:1], None, ALU.mult).then_inc(acc_ready, 1)
                dve.wait_ge(hi_ready, m + 1)
                dve.tensor_tensor(lo[0][:, m, :], x[:, m, :], hi[0][:, m, :].bitcast(F32), ALU.subtract)\
                    .then_inc(lo_ready, 1)
            for t in range(NT):
                link(dve.tensor_scalar(cur[:, t % 2, :], count[t], 0.0, None, ALU.is_gt))
                link(dve.tensor_reduce(out_deg[:, t:t + 1], cur[:, t % 2, :], AX.X, ALU.add))
            dve.tensor_scalar(out_deg[:], out_deg[:], 1.0, None, ALU.add).then_inc(deg_ready, 1)
            dve.wait_ge(deg_root_ready, 1)
            dve.reciprocal(inv_root[:], deg_root[:]).then_inc(gcn_adj_ready, 1)
            for i in range(1, HOPS + 1):
                for m in range(NT):
                    if i < HOPS:
                        dve.wait_ge(hi_ready, i * NT + m + 1)
                        dve.scalar_tensor_tensor(lo[i % 2][:, m, :], main[m][:], inv_row[:, m:m + 1],
                                                 hi[i % 2][:, m, :].bitcast(F32), ALU.mult, ALU.subtract).then_inc(lo_ready, 1)
                    else:
                        dve.wait_ge(hop_ready, (i - 1) * NT + m + 1)
                    dve.wait_ge(acc_ready, (i - 1) * NT + m + 1)
                    dve.scalar_tensor_tensor(h[:, m, :], main[m][:], dw_inv[:, i - 1, m:m + 1], h[:, m, :], ALU.mult, ALU.add)\
                        .then_inc(acc_ready, 1)
                    if i == HOPS:
                        dve.wait_ge(acc_ready, i * NT + m + 1)
                        dve.wait_ge(x_again_loaded, 16)
                        link(dve.scalar_tensor_tensor(x[:, m, :], h[:, m, :], 0.0, x[:, m, :], ALU.max, ALU.add))
                        moments(TO_REL, m, x[:, m, :])
                        scale_and_shift(TO_REL, m)
            dve.wait_ge(wgt_deg_ready, 1)
            link(dve.tensor_scalar(wgt_deg[:], cnt_bank[:, 0:NT], 1.0, None, ALU.max))
            dve.reciprocal(inv_wgt[:], wgt_deg[:]).then_inc(wgt_deg_out, 1)
            for m in range(NT):
                dve.wait_ge(self_ready, m + 1)
                dve.wait_ge(self_biased, m + 1)
                dve.tensor_tensor(h[:, m, :], main[m][:], h[:, m, :], ALU.add).then_inc(self_out, 1)
            dve.wait_ge(rel_rows_loaded, 16 * R)
            for r in range(R):
                for m in range(NT):
                    dve.wait_ge(msg_ready, r * NT + m + 1)
                    dve.tensor_tensor(msg[r][:, m, :], main[m][:], brel[r], ALU.add).then_inc(msg_out, 1)
            dve.wait_ge(wgt_deg_out, 1)
            for m in range(NT):
                dve.wait_ge(agg_ready, m + 1)
                dve.wait_ge(self_out, m + 1)
                dve.scalar_tensor_tensor(h[:, m, :], main[m][:], inv_wgt[:, m:m + 1], h[:, m, :], ALU.mult, ALU.add)\
                    .then_inc(agg_out, 1)
                dve.wait_ge(agg_out, m + 1)
                moments(MID, m, h[:, m, :])
                affine_norm(MID, m, h[:, m, :], g1, be1, h[:, m, :]).then_inc(h_ready[MID], 1)
            for m in range(NT):
                dve.wait_ge(down_ready, m + 1)
                dve.wait_ge(ffn_biased, m + 1)
                dve.tensor_tensor(h[:, m, :], main[m][:], h[:, m, :], ALU.add).then_inc(down_out, 1)
                dve.wait_ge(down_out, m + 1)
                moments(OUT_FFN, m, h[:, m, :])
                dve.wait_ge(ln2_biased, m + 1)
                link(affine_norm(OUT_FFN, m, h[:, m, :], g2, x[:, m, :], x[:, m, :]))
                moments(TO_GCN, m, x[:, m, :])
                scale_and_shift(TO_GCN, m)
            for t in range(NT):
                dve.wait_ge(cnt_t_ready, NT + t + 1)
                half = misc_bank if t % 2 else cnt_bank
                dve.scalar_tensor_tensor(adj[:, t, :], half[:], 0.0, eye_of(t), ALU.is_gt, ALU.add).then_inc(cnt_t_out, 1)
            for m in range(NT):
                dve.wait_ge(sup_hi, m + 1)
                dve.scalar_tensor_tensor(lo[0][:, m, :], main[m][:], inv_root[:, m:m + 1], hi[0][:, m, :].bitcast(F32),
                                         ALU.mult, ALU.subtract).then_inc(sup_out, 1)
            for m in range(NT):
                dve.wait_ge(gcn_ready, m + 1)
                dve.wait_ge(gcn_biased, m + 1)
                dve.scalar_tensor_tensor(x[:, m, :], main[m][:], inv_root[:, m:m + 1], x[:, m, :], ALU.mult, ALU.add)\
                    .then_inc(gcn_out, 1)
                dve.wait_ge(gcn_out, m + 1)
                moments(TO_SAGE, m, x[:, m, :])
                scale_and_shift(TO_SAGE, m)
            dve.wait_ge(cnt_ready, 1)
            link(dve.tensor_scalar(inv_cnt[:], cnt_bank[:], 1.0, None, ALU.max))
            link(dve.reciprocal(inv_cnt[:], inv_cnt[:]))
            for layer in range(2):
                for k in range(KT):
                    dve.wait_ge(mean_ready[layer], k + 1)
                    dve.tensor_tensor(agg_t[layer][:, k, :], main[k][:], inv_cnt[:], ALU.mult).then_inc(mean_out[layer], 1)
                for m in range(NT):
                    dve.wait_ge(sage_ready[layer], m + 1)
                    if layer == 0:
                        dve.wait_ge(late_rows_loaded, 16 * 3)
                        dve.tensor_tensor(h[:, m, :], main[m][:], bl1, ALU.add).then_inc(sage_out[0], 1)
                    else:
                        dve.wait_ge(sage_biased, m + 1)
                        dve.tensor_tensor(x[:, m, :], main[m][:], x[:, m, :], ALU.add).then_inc(sage_out[1], 1)

        @block.tensor
        def _(pe):
            def fill(use, blocks):
                if use >= 2:
                    pe.wait_ge(t_out, use - 1)
                for i, b in enumerate(blocks):
                    ins = pe.transpose(t_bank[use % 2][:, i * P:(i + 1) * P], b, ident[:])
                ins.then_inc(t_ready, 1)

            def fill_h(what, t, ready):
                pe.wait_ge(ready, t + 1)
                fill(use_of(what, t), [h[:, t, k * P:(k + 1) * P] for k in range(KT)])

            def fill_sage(what, q, k):
                pe.wait_ge(sage_loaded[q], 16)
                fill(use_of(what, k), [sage_raw[q][:, o, k * P:(k + 1) * P] for o in range(KT)])

            def product(bank, pairs):
                for i, (left, right) in enumerate(pairs):
                    ins = pe.matmul(bank[:], left, right, start=(i == 0), stop=(i == len(pairs) - 1))
                return ins

            def rows_by(weight, m):
                return [(h_t[:, k, m * P:(m + 1) * P], weight[:, k, :]) for k in range(KT)]

            def transpose_then(what, ready, each):
                fill_h(what, 0, ready)
                for t in range(NT):
                    if t + 1 < NT:
                        fill_h(what, t + 1, ready)
                    pe.wait_ge(t_out, use_of(what, t) + 1)
                    each(t)

            def transpose_counts(base):
                for t in range(NT):
                    n = base + t
                    if t >= 2:
                        pe.wait_ge(cnt_t_out, n - 1)
                    bank = misc_bank if t % 2 else cnt_bank
                    for s in range(NT):
                        ins = pe.transpose(bank[:, s * P:(s + 1) * P], count[s][:, t * P:(t + 1) * P], ident[:])
                    ins.then_inc(cnt_t_ready, 1)

            transpose_counts(0)
            for i in range(1, HOPS + 1):
                src = (i - 1) % 2
                pe.wait_ge(cnt_t_out, NT)
                pe.wait_ge(lo_ready, i * NT)
                pe.wait_ge(acc_ready, i * NT)
                for m in range(NT):
                    cols = slice(m * P, (m + 1) * P)
                    pairs = [(adj[:, s, cols], part[src][:, s, :]) for part in (hi, lo) for s in range(NT)]
                    product(main[m], pairs).then_inc(hop_ready, 1)
            pe.wait_ge(wgt_add, R - 1)
            for m in range(NT):
                for s in range(NT):
                    ins = pe.matmul(cnt_bank[:, m:m + 1], wgt_sum[:, s, m * P:(m + 1) * P], ones[:, 0:1],
                                    start=(s == 0), stop=(s == NT - 1))
            ins.then_inc(wgt_deg_ready, 1)
            pe.wait_ge(wself_loaded, 16)

            def by_self(m):
                pe.wait_ge(acc_ready, HOPS * NT + m + 1)
                product(main[m], rows_by(wself, m)).then_inc(self_ready, 1)

            transpose_then(H1, h_ready[TO_REL], by_self)
            for r in range(R):
                pe.wait_ge(wrel_loaded[r], 16)
                for m in range(NT):
                    if r == 0:
                        pe.wait_ge(self_out, m + 1)
                    else:
                        pe.wait_ge(msg_out, (r - 1) * NT + m + 1)
                    product(main[m], rows_by(wrel[r], m)).then_inc(msg_ready, 1)
            pe.wait_ge(msg_out, R * NT)
            for m in range(NT):
                cols = slice(m * P, (m + 1) * P)
                pairs = [(wall[:, s, r, cols], msg[r][:, s, :]) for r in range(R) for s in range(NT)]
                product(main[m], pairs).then_inc(agg_ready, 1)
            for t in range(NT):
                fill_h(H2, t, h_ready[MID])
            pe.wait_ge(t_out, use_of(H2, NT - 1) + 1)
            pe.wait_ge(wf1_loaded, 16)
            for g in range(GT):
                if g < 4:
                    pe.wait_ge(agg_out, g + 1)
                else:
                    pe.wait_ge(up_out, g - 3)
                pairs = [(wf1[:, k, g * P:(g + 1) * P], h_t[:, k, :]) for k in range(KT)]
                product(main[g % 4], pairs).then_inc(up_ready, 1)
            pe.wait_ge(up_out, GT)
            pe.wait_ge(wf2_loaded, 16)
            for m in range(NT):
                pairs = [(hid[:, g, m * P:(m + 1) * P], wf2[:, g, :]) for g in range(GT)]
                product(main[m], pairs).then_inc(down_ready, 1)
                fill_sage(WL1, 0, m)
            pe.wait_ge(wgt_deg_out, 1)
            transpose_counts(NT)
            pe.wait_ge(w2_loaded, 16)
            for t in range(NT):
                fill_h(H3, t, h_ready[TO_GCN])
            for m in range(NT):
                pe.wait_ge(t_out, use_of(H3, m) + 1)
                pe.wait_ge(down_out, m + 1)
                product(main[m], rows_by(w2, m)).then_inc(sup_ready, 1)
                fill_sage(WR1, 1, m)
            pe.wait_ge(cnt_t_out, 2 * NT)
            pe.wait_ge(sup_out, NT)
            for m in range(NT):
                cols = slice(m * P, (m + 1) * P)
                pairs = [(adj[:, s, cols], part[0][:, s, :]) for part in (hi, lo) for s in range(NT)]
                product(main[m], pairs).then_inc(gcn_ready, 1)
                fill_sage(WL2, 2, m)
            product(cnt_bank, [(ones[:], count[s]) for s in range(NT)]).then_inc(cnt_ready, 1)
            for layer in range(2):
                if layer == 0:
                    for t in range(NT):
                        fill_h(H4, t, h_ready[TO_SAGE])
                    pe.wait_ge(gcn_out, NT)
                else:
                    for t in range(NT):
                        fill_h(H5, t, relu_ready)
                for k in range(KT):
                    pairs = [(h[:, s, k * P:(k + 1) * P], count[s]) for s in range(NT)]
                    product(main[k], pairs).then_inc(mean_ready[layer], 1)
                    if layer == 0:
                        fill_sage(WR2, 3, k)
                pe.wait_ge(mean_out[layer], KT)
                wl, wr = 2 * layer, 2 * layer + 1
                what = H5 if layer else H4
                pe.wait_ge(t_out, use_of(what if layer else WR2, NT - 1) + 1)
                for m in range(NT):
                    cols = slice(m * P, (m + 1) * P)
                    pairs = [(agg_t[layer][:, k, cols], sage(wl, k)) for k in range(KT)]
                    pairs += [(h_t[:, k, cols], sage(wr, k)) for k in range(KT)]
                    product(main[m], pairs).then_inc(sage_ready[layer], 1)


_INS = ['x', 'src', 'dst', 'edge_type_4', 'edge_weight', 'L0_gnn_W', 'L0_gnn_b', 'L0_gnn_diffusion_weights',
        'L1_gnn_W_self', 'L1_gnn_b_self', 'L1_gnn_W_rel', 'L1_gnn_b_rel', 'L1_gnn_ln1_g', 'L1_gnn_ln1_b', 'L1_gnn_ln2_g',
        'L1_gnn_ln2_b', 'L1_gnn_W_ffn1', 'L1_gnn_b_ffn1', 'L1_gnn_W_ffn2', 'L1_gnn_b_ffn2', 'L2_gnn_weight', 'L2_gnn_bias',
        'L3_gnn_Wl1', 'L3_gnn_bl1', 'L3_gnn_Wr1', 'L3_gnn_Wl2', 'L3_gnn_bl2', 'L3_gnn_Wr2']


def kernel(**inputs):
    import numpy as _np
    import concourse.bacc as _bacc
    from concourse import mybir as _mybir
    from concourse.bass_utils import run_bass_kernel_spmd as _run

    nc = _bacc.Bacc("TRN2", target_bir_lowering=False, num_devices=1)
    arrays, args = {}, []
    for name in _INS:
        a = _np.ascontiguousarray(inputs[name])
        arrays[f"in_{name}"] = a
        args.append(nc.dram_tensor(f"in_{name}", a.shape, _mybir.dt.from_np(a.dtype), kind="ExternalInput").ap())
    args.append(nc.dram_tensor("out", (N, D), F32, kind="ExternalOutput").ap())
    gnn_program(nc, *args)
    r = _run(nc, [arrays], core_ids=[0])
    return r.results[0]["out"]
```

```python
from contextlib import ExitStack

import concourse.bass as bass
from concourse import mybir

F32 = mybir.dt.float32
F32R = mybir.dt.float32r
BF16 = mybir.dt.bfloat16
F16 = mybir.dt.float16
I32 = mybir.dt.int32
ALU = mybir.AluOpType
ACT = mybir.ActivationFunctionType
AX = mybir.AxisListType
PE, DVE = mybir.EngineType.PE, mybir.EngineType.DVE

P = 128
N = 512
D = 512
E = 16384
R = 4
NT = N // P
KT = D // P
CH = E // P
V = 3
WD = P // (V * R + 1)
NW = -(-N // WD)
WC = 4
WK = R * WD
WM = V * WK + WD
OUT_R = R + 1
GROUP = 4
UNROLL = 2 * GROUP
RING = UNROLL
LAST = NW - 1
LEAD = CH // 8
PACE = (CH - LEAD) // LAST
F1 = 2 * D
GT = F1 // P
EPS = 1e-5
HOPS = 3
assert N == D and WM <= P and LAST % UNROLL == 0 and LEAD + PACE * LAST == CH and E % P == 0


def gnn_program(nc, x_in, src_in, dst_in, typ_in, wgt_in, w0_in, b0_in, dw_in, wself_in, bself_in, wrel_in, brel_in,
                g1_in, be1_in, g2_in, be2_in, wf1_in, bf1_in, wf2_in, bf2_in, w2_in, b2_in,
                wl1_in, bl1_in, wr1_in, wl2_in, bl2_in, wr2_in, out):
    with ExitStack() as keep:
        def sem(name):
            return keep.enter_context(nc.semaphore(name))

        def sb(name, shape, dt):
            return keep.enter_context(nc.sbuf_tensor(name, shape, dt))

        wall = sb("wall", [P, OUT_R, NT, N], F32)
        x = sb("x", [P, NT, D], F32)
        ident = sb("ident", [P, P], F32)
        ones = sb("ones", [P, P], F32)
        psum = [keep.enter_context(nc.psum_tensor(f"bank{i}", [P, 512], F32)) for i in range(8)]
        eye = sb("eye", [P, 2 * N - P], BF16)
        eps = sb("eps", [P, 1], F32)
        slow_flag = sb("slow_flag", [P, 1], I32)

        def load_flag(engine, kind):
            return engine.to_reg(nc.values_load_multi_w_load_instructions(
                slow_flag[0:1, 0:1], [kind], min_val=0, max_val=1,
                skip_runtime_bounds_check_because="the chip writes 0 or 1")[1][0])

        build_matrices(nc, sem, wall, x, ident, ones, eye, eps, slow_flag, load_flag, psum, x_in, src_in, dst_in, typ_in,
                       wgt_in, w0_in, b0_in)
        run_blocks(nc, sem, wall, x, ident, ones, eye, eps, load_flag, psum, x_in, dw_in, wself_in, bself_in, wrel_in, brel_in,
                   g1_in, be1_in, g2_in, be2_in, wf1_in, bf1_in, wf2_in, bf2_in, w2_in, b2_in,
                   wl1_in, bl1_in, wr1_in, wl2_in, bl2_in, wr2_in, out)


def build_matrices(nc, sem, wall, x, ident, ones, eye, eps, slow_flag, load_flag, psum, x_in, src_in, dst_in, typ_in,
                   wgt_in, w0_in, b0_in):
    with ExitStack() as ctx:
        def sb(name, shape, dt):
            return ctx.enter_context(nc.sbuf_tensor(name, shape, dt))

        src_hot = sb("src_hot", [P, CH, N], BF16)
        win = sb("win", [P, RING, WC, WK + WM], BF16)
        z_sb = sb("z_sb", [P, GROUP, N], F32)
        key_iota = sb("key_iota", [P, R + 1, N], F16)
        key_t = sb("key_t", [P, CH, R + 1], F16)
        src_t = sb("src_t", [P, CH], F32)
        parts = sb("parts", [P, CH, V], F32)
        win_lo = sb("win_lo", [P, NW], F32)
        next_dst_i = sb("next_dst_i", [P, 1], I32)
        next_dst = sb("next_dst", [P, 1], F32)
        viol = sb("viol", [P, 4], F32)
        first_chunk = sb("first_chunk", [P, NW], I32)
        b0 = sb("b0", [P, D], F32)

        whole = wall[:].rearrange("p r t n -> p (r t n)")
        room = [whole[:, i * OUT_R * N:(i + 1) * OUT_R * N] for i in range(NT)]
        iota_i = room[0][:, 0:N].bitcast(I32)
        h_t = z_sb
        w0 = room[2][:, 0:KT * D].rearrange("p (k n) -> p k n", k=KT)
        h = room[3][:, 0:NT * D].rearrange("p (t n) -> p t n", t=NT)
        taken = [0]

        def small(*shape):
            size = 1
            for n in shape:
                size *= n
            ap = room[1][:, taken[0]:taken[0] + size]
            taken[0] += size
            return ap.rearrange("p (a b) -> p a b", a=shape[0]) if len(shape) == 2 else ap

        e_int = small(3, P).bitcast(I32)
        e_wgt = small(P)
        e_f32 = small(3, P)
        wgt_t = small(CH)
        rest = small(2, CH)
        part_b = small(V, CH // 2).bitcast(BF16)
        chunk_cmp = small(2, NW)
        disorder = small(P)
        span = small(3, NW)
        stats = small(NT, 6)
        mean_var = small(NT, 2)
        std, rstd, shift = small(NT), small(NT), small(NT)
        eps_root = small(1)
        slow_src, slow_key, zeros = src_hot[:, 0, :], src_hot[:, 1:2 + V, :], src_hot[:, 2 + V, :]
        slow_key_t = src_hot[:, 3 + V, 0:2 * CH].bitcast(F32)

        dst_loaded, src_loaded, typ_loaded, wgt_loaded = (sem(f"{n}_loaded") for n in ("dst", "src", "typ", "wgt"))
        x_loaded = [sem(f"x{t}_loaded") for t in range(NT)]
        w0_loaded, b0_loaded = sem("w0_loaded"), sem("b0_loaded")
        next_set, next_loaded = sem("next_set"), sem("next_loaded")
        const_set, const_ready = sem("const_set"), sem("const_ready")
        iota_ready, eye_set = sem("iota_ready"), sem("eye_set")
        edges_ready, edges_t_ready = sem("edges_ready"), sem("edges_t_ready")
        cmp_ready, cmp_sum_ready, plan_ready = sem("cmp_ready"), sem("cmp_sum_ready"), sem("plan_ready")
        chain_sem = sem("build_chain")
        var_ready, std_ready, shift_ready, h_ready = sem("var0_ready"), sem("std0_ready"), sem("shift0_ready"), sem("h0_ready")
        t_ready, t_out, proj_ready, proj_out = sem("h0_t_ready"), sem("h0_t_out"), sem("proj_ready"), sem("proj_out")
        proj_biased, counts_t_ready = sem("proj_biased"), sem("counts_t_ready")
        hot_ready, hots_ready, win_ready = sem("hot_ready"), sem("hots_ready"), sem("win_ready")
        z_ready, z_copied, z_t_ready, summed, counted = (
            sem("z_ready"), sem("z_copied"), sem("z_t_ready"), sem("summed"), sem("counted"))
        slow_free, slow_ready, slow_sum, slow_out = sem("slow_free"), sem("slow_ready"), sem("slow_sum"), sem("slow_out")
        slow_cnt, slow_cnt_out, slow_zero = sem("slow_cnt"), sem("slow_cnt_out"), sem("slow_zero")

        z_bank = proj_bank = psum[0:4]
        z_t_bank = psum[4:8]
        t_bank, src_bank, edge_bank, cmp_bank = psum[4:6], psum[3], psum[6], psum[7]
        chunked = "(c e) -> c e"

        def load_starts(kind, w, n):
            return nc.values_load_multi_w_load_instructions(
                first_chunk[0:1, bass.ds(w, n)], [kind], min_val=0, max_val=CH - WC,
                skip_runtime_bounds_check_because="clamped to that on the chip")[1]

        def columns(w):
            return slice(N - WD, N) if w is LAST else bass.ds(w * WD, WD)

        block = ctx.enter_context(nc.Block())

        @block.sync
        def _(sp):
            sp.dma_start(e_int[:, 0, :], dst_in.rearrange(chunked, e=P)).then_inc(dst_loaded, 16)
            for t in range(NT):
                sp.dma_start(x[:, t, :], x_in[t * P:(t + 1) * P, :]).then_inc(x_loaded[t], 16)
                if t == 1:
                    sp.dma_start(e_wgt, wgt_in.rearrange(chunked, e=P)).then_inc(wgt_loaded, 16)
            sp.dma_start(w0, w0_in.rearrange("(k p) n -> p k n", p=P)).then_inc(w0_loaded, 16)

        @block.gpsimd
        def _(pool):
            pool.memset(next_dst_i[:], N).then_inc(next_set, 1)
            pool.wait_ge(next_set, 1)
            pool.dma_start(next_dst_i[0:CH - 1, :], dst_in.rearrange(chunked, e=P)[1:CH, 0:1],
                           allow_slow_non_contiguous=True).then_inc(next_loaded, 16)
            pool.memset(ident[:], 0.0).then_inc(const_set, 1)
            pool.memset(ones[:], 1.0).then_inc(const_ready, 1)
            pool.memset(eps[:], EPS).then_inc(const_ready, 1)
            pool.iota(win_lo[:], pattern=[[WD, NW]], base=0, channel_multiplier=0,
                      allow_small_or_imprecise_dtypes=True).then_inc(const_set, 1)
            pool.wait_ge(const_set, 2)
            pool.memset(win_lo[:, LAST:NW], float(N - WD)).then_inc(const_ready, 1)
            pool.affine_select(out=ident[:], in_=ident[:], compare_op=ALU.not_equal, fill=1.0, base=0,
                               pattern=[[-1, P]], channel_multiplier=1).then_inc(const_ready, 1)
            pool.iota(iota_i, pattern=[[1, N]], base=0, channel_multiplier=0).then_inc(iota_ready, 1)
            pool.dma_start(b0[:], b0_in.partition_broadcast(P)).then_inc(b0_loaded, 16)
            pool.memset(eye[:], 0.0).then_inc(eye_set, 1)
            pool.wait_ge(eye_set, 1)
            pool.affine_select(out=eye[:], in_=eye[:], compare_op=ALU.not_equal, fill=1.0, base=N - P,
                               pattern=[[-1, 2 * N - P]], channel_multiplier=1).then_inc(eye_set, 1)
            pool.wait_ge(plan_ready, 2)
            slow = load_flag(pool, mybir.EngineType.Pool)

            def weigh(w, n):
                starts = load_starts(mybir.EngineType.Pool, w, n)
                for j in range(n):
                    pool.wait_ge(hots_ready, w + j + 1)
                    hot = win[:, j, :, 0:WK].unsqueeze(2).broadcast_to([P, WC, V, WK])
                    wgt = parts[:, bass.ds(starts[j], WC), :].unsqueeze(3).broadcast_to([P, WC, V, WK])
                    pool.tensor_tensor(win[:, j, :, WK + WD:].rearrange("p c (v k) -> p c v k", v=V), hot, wgt, ALU.mult)\
                        .then_inc(win_ready, 1)

            with pool.If_eq(slow, 0):
                weigh(0, UNROLL)
                with pool.Fori(1, LAST // UNROLL) as i:
                    weigh(i * UNROLL, UNROLL)
                weigh(LAST, 1)

            pool.wait_ge(b0_loaded, 16)
            for m in range(NT):
                pool.wait_ge(proj_out, m + 1)
                pool.tensor_tensor(x[:, m, :], x[:, m, :], b0[:], ALU.add).then_inc(proj_biased, 1)

        @block.scalar
        def _(act):
            act.dma_start(e_int[:, 1, :], src_in.rearrange(chunked, e=P)).then_inc(src_loaded, 16)
            act.dma_start(e_int[:, 2, :], typ_in.rearrange(chunked, e=P)).then_inc(typ_loaded, 16)
            act.wait_ge(const_ready, 4)
            act.activation(eps_root, eps[:], ACT.Sqrt)
            def empty(t):
                act.wait_ge(t_ready, t + 1)
                act.activation(h_t[:, :, t * P:(t + 1) * P], t_bank[t % 2][:].rearrange("p (k n) -> p k n", k=KT),
                               ACT.Copy).then_inc(t_out, 1)

            for t in range(NT):
                act.wait_ge(var_ready, t + 1)
                act.activation(std[:, t:t + 1], mean_var[:, t, 1:2], ACT.Sqrt, bias=eps[:]).then_inc(std_ready, 1)
                if t > 0:
                    empty(t - 1)
                act.wait_ge(shift_ready, t + 1)
                act.activation(h[:, t, :], x[:, t, :], ACT.Relu, bias=shift[:, t:t + 1], scale=rstd[:, t:t + 1])\
                    .then_inc(h_ready, 1)
            empty(NT - 1)
            for m in range(NT):
                act.wait_ge(proj_ready, m + 1)
                act.activation(x[:, m, :], proj_bank[m][:], ACT.Copy).then_inc(proj_out, 1)
            act.wait_ge(plan_ready, 2)
            slow = load_flag(act, mybir.EngineType.Activation)

            def copy_sums(first, w, k):
                act.wait_ge(z_ready, w + 1)
                if not first:
                    act.wait_ge(z_t_ready, w - GROUP + 1)
                act.activation(z_sb[0:WM, k, :], z_bank[k][0:WM, :], ACT.Copy).then_inc(z_copied, 1)

            def copy_counts(w, k):
                act.wait_ge(summed, w + 1)
                got = z_t_bank[k][:, 0:NT * WD].rearrange("p (t d) -> p t d", t=NT)
                act.activation(wall[:, R, :, columns(w)], got, ACT.Copy).then_inc(counted, 1)

            def pass_of_windows(first, i):
                for side in range(2):
                    w0 = i * UNROLL + side * GROUP
                    if not first:
                        for k in range(GROUP):
                            copy_counts(w0 - 2 * GROUP + k, k)
                    for k in range(GROUP):
                        copy_sums(first and side == 0, w0 + k, k)

            with act.If_eq(slow, 0):
                pass_of_windows(True, 0)
                with act.Fori(1, LAST // UNROLL) as i:
                    pass_of_windows(False, i)
                for k in range(GROUP):
                    copy_counts(LAST - 2 * GROUP + k, k)
                copy_sums(False, LAST, 0)
                for k in range(GROUP):
                    copy_counts(LAST - GROUP + k, k)
                act.wait_ge(counted, LAST)
                copy_counts(LAST, 0)

        @block.vector
        def _(dve):
            links = [0]

            def link(*steps):
                for ins in steps:
                    links[0] += 1
                    ins.then_inc(chain_sem, 1)
                dve.wait_ge(chain_sem, links[0])

            dve.wait_ge(dst_loaded, 16)
            dve.tensor_copy(e_f32[:, 0, :], e_int[:, 0, :]).then_inc(edges_ready, 1)
            dve.wait_ge(iota_ready, 1)
            dve.tensor_copy(key_iota[:, 0, :], iota_i).then_inc(iota_ready, 1)
            dve.wait_ge(src_loaded, 16)
            dve.tensor_copy(e_f32[:, 1, :], e_int[:, 1, :]).then_inc(edges_ready, 1)
            dve.wait_ge(iota_ready, 2)
            for r in range(1, R + 1):
                dve.tensor_scalar(key_iota[:, r, :], key_iota[:, 0, :], float(r % R * N), None, ALU.add).then_inc(iota_ready, 1)
            dve.wait_ge(typ_loaded, 16)
            dve.scalar_tensor_tensor(e_f32[:, 2, :], e_int[:, 2, :], float(N), e_int[:, 0, :], ALU.mult, ALU.add)\
                .then_inc(edges_ready, 1)

            def moments(t):
                dve.wait_ge(x_loaded[t], 16)
                link(dve.bn_stats(stats[:, t, :], x[:, t, :]))
                dve.bn_aggr(mean_var[:, t, :], stats[:, t, :]).then_inc(var_ready, 1)

            def scale_and_shift(t):
                dve.wait_ge(std_ready, t + 1)
                link(dve.reciprocal(rstd[:, t:t + 1], std[:, t:t + 1]))
                dve.tensor_scalar(shift[:, t:t + 1], mean_var[:, t, 0:1], rstd[:, t:t + 1], -1.0, ALU.mult, ALU.mult)\
                    .then_inc(shift_ready, 1)

            moments(0)
            dve.wait_ge(edges_ready, 1)
            dve.wait_ge(const_ready, 3)
            dve.tensor_scalar(chunk_cmp[:, 0, :], win_lo[:], e_f32[:, 0, P - 1:P], None, ALU.is_gt).then_inc(cmp_ready, 1)
            link(dve.tensor_scalar(span[:, 0, :], win_lo[:], float(WD), None, ALU.add))
            dve.tensor_scalar(chunk_cmp[:, 1, :], span[:, 0, :], e_f32[:, 0, 0:1], None, ALU.is_gt).then_inc(cmp_ready, 1)
            scale_and_shift(0)
            moments(1)
            dve.wait_ge(next_loaded, 16)
            link(dve.tensor_copy(next_dst[:], next_dst_i[:]))
            dve.tensor_tensor(viol[:, 1:2], e_f32[:, 0, P - 1:P], next_dst[:], ALU.is_gt).then_inc(cmp_ready, 1)
            link(dve.tensor_tensor(disorder[:, 0:P - 1], e_f32[:, 0, 0:P - 1], e_f32[:, 0, 1:P], ALU.is_gt))
            dve.tensor_reduce(viol[:, 0:1], disorder[:, 0:P - 1], AX.X, ALU.add).then_inc(cmp_ready, 1)
            scale_and_shift(1)

            def source_hot(n):
                dve.tensor_scalar(src_hot[:, bass.ds(n, 1), :].squeeze(1), key_iota[:, 0, :], src_t[:, bass.ds(n, 1)], None,
                                  ALU.is_equal).then_inc(hot_ready, 1)

            dve.wait_ge(edges_t_ready, 1)
            dve.tensor_copy(src_t[:], src_bank[:, 0:P]).then_inc(edges_ready, 1)
            dve.wait_ge(edges_ready, 4)
            for t in range(2, NT):
                moments(t)
                for c in range((t - 2) * LEAD // 4, (t - 1) * LEAD // 4):
                    source_hot(c)
                scale_and_shift(t)
            dve.wait_ge(edges_t_ready, 4)
            dve.tensor_copy(key_t[:, :, 0:R], edge_bank[:, P:2 * P].unsqueeze(2).broadcast_to([P, CH, R]))\
                .then_inc(edges_ready, 1)
            dve.tensor_copy(key_t[:, :, R], edge_bank[:, 3 * P:4 * P]).then_inc(edges_ready, 1)
            link(dve.tensor_copy(wgt_t, edge_bank[:, 2 * P:3 * P]))
            dve.wait_ge(cmp_sum_ready, 1)
            link(dve.tensor_copy(part_b[:, 0, :], wgt_t),
                 dve.tensor_scalar(span[:, 0, :], cmp_bank[:, 0:NW], float(CH - WC), None, ALU.min))
            dve.tensor_copy(first_chunk[:], span[:, 0, :]).then_inc(plan_ready, 1)
            link(dve.tensor_tensor(rest[:, 0, :], wgt_t, part_b[:, 0, :], ALU.subtract),
                 dve.scalar_tensor_tensor(span[:, 2, :], win_lo[:], -float(PACE) / WD, span[:, 0, :], ALU.mult, ALU.add),
                 dve.tensor_tensor(span[:, 1, :], cmp_bank[:, NW:2 * NW], span[:, 0, :], ALU.subtract),
                 dve.tensor_copy(viol[:, 3:4], cmp_bank[:, 2 * NW:2 * NW + 1]))
            link(dve.tensor_copy(part_b[:, 1, :], rest[:, 0, :]),
                 dve.scalar_tensor_tensor(span[:, 2, :], span[:, 2, :], float(LEAD + PACE - 2 * WC), span[:, 1, :],
                                          ALU.subtract, ALU.max))
            link(dve.tensor_tensor(rest[:, 1, :], rest[:, 0, :], part_b[:, 1, :], ALU.subtract),
                 dve.tensor_scalar(span[:, 2, :], span[:, 2, :], float(WC), None, ALU.is_gt))
            link(dve.tensor_copy(part_b[:, 2, :], rest[:, 1, :]),
                 dve.tensor_reduce(viol[:, 2:3], span[:, 2, :], AX.X, ALU.add))
            link(dve.tensor_tensor(span[:, 1, 0:1], viol[:, 2:3], viol[:, 3:4], ALU.add),
                 dve.tensor_copy(parts[:].rearrange("p c v -> p v c"), part_b))
            dve.tensor_scalar(slow_flag[:], span[:, 1, 0:1], 0.0, None, ALU.is_gt).then_inc(plan_ready, 1)
            dve.wait_ge(plan_ready, 2)
            slow = load_flag(dve, DVE)
            dve.wait_ge(iota_ready, R + 2)
            dve.wait_ge(edges_ready, 6)

            def window(first, w, place, start):
                if w is not LAST:
                    for c in range(PACE):
                        source_hot(w * PACE + LEAD + c)
                if not first:
                    dve.wait_ge(z_ready, w - RING + 1)
                here = bass.ds(start, WC)
                key = key_t[:, here, :].unsqueeze(3).broadcast_to([P, WC, R + 1, WD])
                want = key_iota[:, :, columns(w)].unsqueeze(1).broadcast_to([P, WC, R + 1, WD])
                dve.tensor_tensor(win[:, place, :, 0:WK + WD].rearrange("p c (r d) -> p c r d", d=WD), key, want, ALU.is_equal)\
                    .then_inc(hots_ready, 1)

            def sum_parts(w, k):
                dve.wait_ge(z_t_ready, w + 1)
                got = z_t_bank[k][:, NT * WD:NT * WM].rearrange("p (v r d) -> p r d v", v=V, d=WD)
                dve.tensor_reduce(wall[:, 0:R, :, columns(w)].rearrange("p r t d -> p (r t) d"),
                                  got, AX.X, ALU.add).then_inc(summed, 1)

            def pass_of_windows(first, sums, i):
                starts = load_starts(DVE, i * UNROLL, UNROLL)
                for side in range(2):
                    if side >= sums:
                        for k in range(GROUP):
                            sum_parts(i * UNROLL + (side - 3) * GROUP + k, k)
                    for j in range(side * GROUP, (side + 1) * GROUP):
                        window(first, i * UNROLL + j, j, starts[j])

            with dve.If_eq(slow, 0):
                for c in range(LEAD // 2, LEAD):
                    source_hot(c)
                pass_of_windows(True, 2, 0)
                pass_of_windows(False, 1, 1)
                with dve.Fori(2, LAST // UNROLL) as i:
                    pass_of_windows(False, 0, i)
                start, = load_starts(DVE, LAST, 1)
                for k in range(GROUP):
                    sum_parts(LAST - 3 * GROUP + k, k)
                window(False, LAST, 0, start)
                for w in range(LAST - 2 * GROUP, LAST):
                    sum_parts(w, w % GROUP)
                dve.wait_ge(summed, LAST)
                sum_parts(LAST, 0)

            with dve.If_ne(slow, 0):
                dve.wait_ge(hot_ready, LEAD // 2)
                link(dve.tensor_copy(slow_key_t, key_t[:, :, 0]))
                dve.memset(zeros, 0.0).then_inc(slow_zero, 1)
                dve.memset(slow_src, 0.0).then_inc(slow_free, 1)
                with dve.Fori(0, R) as r:
                    with dve.Fori(0, CH) as c:
                        dve.wait_ge(slow_free, r * CH + c + 1)
                        dve.tensor_scalar(slow_src, key_iota[:, 0, :], src_t[:, bass.ds(c, 1)], None, ALU.is_equal)\
                            .then_inc(slow_ready, 1)
                        for v in range(V):
                            dve.tensor_scalar(slow_key[:, v, :], key_iota[:, bass.ds(r, 1), :].squeeze(1),
                                              slow_key_t[:, bass.ds(c, 1)], parts[:, bass.ds(c, 1), v], ALU.is_equal, ALU.mult)\
                                .then_inc(slow_ready, 1)
                        dve.tensor_scalar(slow_key[:, V, :], key_iota[:, bass.ds(r, 1), :].squeeze(1),
                                          slow_key_t[:, bass.ds(c, 1)], None, ALU.is_equal).then_inc(slow_ready, 1)
                    dve.wait_ge(slow_sum, r + 1)
                    for t in range(NT):
                        dve.tensor_copy(wall[:, bass.ds(r, 1), t, :].squeeze(1), psum[t][:]).then_inc(slow_out, 1)
                dve.wait_ge(slow_cnt, 1)
                for t in range(NT):
                    dve.tensor_copy(wall[:, R, t, :], psum[NT + t][:]).then_inc(slow_cnt_out, 1)

        @block.tensor
        def _(pe):
            pe.wait_ge(const_ready, 4)
            pe.wait_ge(edges_ready, 2)
            pe.transpose(src_bank[:, 0:P], e_f32[:, 1, :], ident[:]).then_inc(edges_t_ready, 1)
            pe.wait_ge(edges_ready, 3)
            pe.transpose(edge_bank[:, P:2 * P], e_f32[:, 2, :], ident[:]).then_inc(edges_t_ready, 1)
            pe.wait_ge(wgt_loaded, 16)
            pe.transpose(edge_bank[:, 2 * P:3 * P], e_wgt, ident[:]).then_inc(edges_t_ready, 1)
            pe.transpose(edge_bank[:, 3 * P:4 * P], e_f32[:, 0, :], ident[:]).then_inc(edges_t_ready, 1)
            def fill_h(t):
                pe.wait_ge(h_ready, t + 1)
                if t >= 2:
                    pe.wait_ge(t_out, t - 1)
                for k in range(KT):
                    ins = pe.transpose(t_bank[t % 2][:, k * P:(k + 1) * P], h[:, t, k * P:(k + 1) * P], ident[:])
                ins.then_inc(t_ready, 1)

            fill_h(0)
            pe.wait_ge(cmp_ready, 4)
            pe.matmul(cmp_bank[:, 0:2 * NW], ones[:], chunk_cmp.rearrange("p a w -> p (a w)"), start=True, stop=True)
            pe.matmul(cmp_bank[:, 2 * NW:2 * NW + 1], ones[:], viol[:, 0:1], start=False, stop=False, skip_group_check=True)
            pe.matmul(cmp_bank[:, 2 * NW:2 * NW + 1], ones[:], viol[:, 1:2], start=False, stop=True, skip_group_check=True)\
                .then_inc(cmp_sum_ready, 1)
            pe.wait_ge(w0_loaded, 16)
            for m in range(NT):
                pe.wait_ge(t_out, m + 1)
                if m == NT - 1:
                    pe.wait_ge(edges_ready, 4)
                for k in range(KT):
                    ins = pe.matmul(proj_bank[m][:], h_t[:, k, m * P:(m + 1) * P], w0[:, k, :],
                                    start=(k == 0), stop=(k == KT - 1))
                    if k == KT // 2 - 1 and m + 1 < NT:
                        fill_h(m + 1)
                ins.then_inc(proj_ready, 1)
            pe.wait_ge(plan_ready, 2)
            slow = load_flag(pe, PE)

            def sums(first, w, k, place, start):
                pe.wait_ge(win_ready, w + 1)
                pe.wait_ge(hot_ready, CH if w is LAST else w * PACE + LEAD + PACE)
                if first:
                    pe.wait_ge(proj_out, k + 1)
                else:
                    pe.wait_ge(z_copied, w - GROUP + 1)
                for c in range(WC):
                    ins = pe.matmul(z_bank[k][0:WM, :], win[:, place, c, WK:],
                                    src_hot[:, bass.ds(start + c, 1), :].squeeze(1), start=(c == 0), stop=(c == WC - 1))
                ins.then_inc(z_ready, 1)

            def turn(first, w, k):
                pe.wait_ge(z_copied, w + 1)
                if not first:
                    pe.wait_ge(counted, w - GROUP + 1)
                blocks = z_t_bank[k][:, 0:NT * WM].rearrange("p (b t d) -> p b t d", t=NT, d=WD)
                for t in range(NT):
                    ins = pe.transpose(blocks[:, :, t, :], z_sb[0:WM, k, t * P:(t + 1) * P], ident[0:WM, 0:WM])
                ins.then_inc(z_t_ready, 1)

            def pass_of_windows(first, i):
                starts = load_starts(PE, i * UNROLL, UNROLL)
                for side in range(2):
                    w0 = i * UNROLL + side * GROUP
                    for k in range(GROUP):
                        sums(first and side == 0, w0 + k, k, side * GROUP + k, starts[side * GROUP + k])
                    for k in range(GROUP):
                        if not (first and side == 0):
                            turn(first, w0 - GROUP + k, k)

            def transpose_counts(fast):
                for t in range(NT):
                    if fast:
                        pe.wait_ge(counted, min(NW, -(-(t + 1) * P // WD)))
                    for s in range(NT):
                        ins = pe.transpose(psum[t][:, s * P:(s + 1) * P], wall[:, R, s, t * P:(t + 1) * P], ident[:])
                ins.then_inc(counts_t_ready, 1)

            with pe.If_eq(slow, 0):
                pass_of_windows(True, 0)
                with pe.Fori(1, LAST // UNROLL) as i:
                    pass_of_windows(False, i)
                start, = load_starts(PE, LAST, 1)
                sums(False, LAST, 0, 0, start)
                for k in range(GROUP):
                    turn(False, LAST - GROUP + k, k)
                turn(False, LAST, 0)
                pe.wait_ge(z_copied, NW)
                transpose_counts(True)

            with pe.If_ne(slow, 0):
                pe.wait_ge(proj_out, NT)
                pe.wait_ge(slow_zero, 1)
                for t in range(NT):
                    pe.matmul(psum[NT + t][:], zeros[:, 0:P], zeros, start=True, stop=False)
                with pe.Fori(0, R) as r:
                    for t in range(NT):
                        pe.matmul(psum[t][:], zeros[:, 0:P], zeros, start=True, stop=False)
                    with pe.Fori(0, CH) as c:
                        pe.wait_ge(slow_ready, (r * CH + c + 1) * (V + 2))
                        for t in range(NT):
                            for v in range(V):
                                pe.matmul(psum[t][:], slow_src[:, t * P:(t + 1) * P], slow_key[:, v, :], start=False, stop=False)
                            ins = pe.matmul(psum[NT + t][:], slow_src[:, t * P:(t + 1) * P], slow_key[:, V, :],
                                            start=False, stop=False)
                        ins.then_inc(slow_free, 1)
                    for t in range(NT):
                        ins = pe.matmul(psum[t][:], zeros[:, 0:P], zeros, start=False, stop=True)
                    ins.then_inc(slow_sum, 1)
                    pe.wait_ge(slow_out, r * NT + NT)
                for t in range(NT):
                    ins = pe.matmul(psum[NT + t][:], zeros[:, 0:P], zeros, start=False, stop=True)
                ins.then_inc(slow_cnt, 1)
                pe.wait_ge(slow_cnt_out, NT)
                transpose_counts(False)


H_REL, H_FFN, H_GCN, H_SAGE1, H_SAGE2, WL1, WR1, WL2, WR2 = range(9)
FILLS = ([(H_REL, t) for t in range(NT)] + [(H_FFN, t) for t in range(NT)] + [(WL1, t) for t in range(NT)]
         + [(WR1, t) for t in range(NT)] + [(WL2, 0)] + [(H_GCN, t) for t in range(NT)] + [(WL2, t) for t in range(1, NT)]
         + [(what, t) for what in (H_SAGE1, WR2, H_SAGE2) for t in range(NT)])


def use_of(what, t):
    return FILLS.index((what, t))


def run_blocks(nc, sem, wall, x, ident, ones, eye, eps, load_flag, psum, x_in, dw_in, wself_in, bself_in, wrel_in, brel_in,
               g1_in, be1_in, g2_in, be2_in, wf1_in, bf1_in, wf2_in, bf2_in, w2_in, b2_in,
               wl1_in, bl1_in, wr1_in, wl2_in, bl2_in, wr2_in, out):
    with ExitStack() as ctx:
        def sb(name, shape, dt):
            return ctx.enter_context(nc.sbuf_tensor(name, shape, dt))

        slots = sb("slots", [P, 8, KT * D], F32)

        def place(n, k=KT):
            return slots[:, n:n + k // KT, :].rearrange("p a (k n) -> p (a k) n", k=KT)

        wself, wrel = place(1), [place(2 + r) for r in range(R)]
        msg = [place(6), place(7), place(0), place(1)]
        wgt_sum = place(7)
        wf1 = slots[:, 2:4, :].rearrange("p a n -> p (a n)").rearrange("p (k n) -> p k n", k=KT)
        wf2 = place(4, GT)
        hid = place(6, GT)
        w2 = place(0)
        sage_raw = [place(1), place(2), place(3), place(4)]
        agg_t = [place(6), place(7)]

        def sage(q, k):
            return wall[:, q, k, :]

        count = [wall[:, R, t, :] for t in range(NT)]
        h = sb("h", [P, NT, D], F32)
        h_t = sb("h_t", [P, KT, N], F32)
        adj = sb("adj", [P, NT, N], F32R)
        hi = [sb(f"hi{i}", [P, NT, D], F32R) for i in range(2)]
        lo = [sb(f"lo{i}", [P, NT, D], F32R) for i in range(2)]
        cnt_r = sb("cnt_r", [P, NT, N], F32R)
        both_ways = sb("both_ways", [P, 2, N], F32)
        bias = sb("bias", [P, 6 + R, D], F32)
        bself, g1, be1, g2, be2, bf2 = (bias[:, i, :] for i in range(6))
        brel = [bias[:, 6 + r, :] for r in range(R)]
        b2, bl1, bl2 = (bias[:, 6 + i, :] for i in range(3))
        bf1 = sb("bf1", [P, GT], F32)
        dw = sb("dw", [P, HOPS + 1], F32)
        dw_inv = sb("dw_inv", [P, HOPS, NT], F32)
        stats = sb("stats", [P, NT, 6], F32)
        mean_var = sb("mean_var", [P, NT, 2], F32)
        std = sb("std", [P, NT], F32)
        rstd = sb("rstd", [P, NT], F32)
        shift = sb("shift", [P, NT], F32)
        row_sum = sb("row_sum", [P, NT], F32)
        inv_row = sb("inv_row", [P, NT], F32)
        out_deg = sb("out_deg", [P, NT], F32)
        deg_root = sb("deg_root", [P, NT], F32)
        inv_root = sb("inv_root", [P, NT], F32)
        wgt_deg = sb("wgt_deg", [P, NT], F32)
        inv_wgt = sb("inv_wgt", [P, NT], F32)
        inv_cnt = sb("inv_cnt", [P, N], F32)

        rows_loaded, rel_rows_loaded, late_rows_loaded = sem("rows_loaded"), sem("rel_rows_loaded"), sem("late_rows_loaded")
        dw_loaded, bf1_loaded = sem("dw_loaded"), sem("bf1_loaded")
        x_again_loaded, wself_loaded, w2_loaded = sem("x_again_loaded"), sem("wself_loaded"), sem("w2_loaded")
        wrel_loaded = [sem(f"wrel{r}_loaded") for r in range(R)]
        wf1_loaded, wf2_loaded = sem("wf1_loaded"), sem("wf2_loaded")
        sage_loaded = [sem(f"sage{q}_loaded") for q in range(4)]
        out_stored = sem("out_stored")
        cnt_r_ready = sem("cnt_r_ready")
        wgt_add, self_biased, ffn_biased, ln2_biased = sem("wgt_add"), sem("self_biased"), sem("ffn_biased"), sem("ln2_biased")
        gcn_biased, sage_biased = sem("gcn_biased"), sem("sage_biased")
        TO_REL, MID, OUT_FFN, TO_GCN, TO_SAGE = range(5)
        NORMS = 5
        var_ready = [sem(f"var_ready{n}") for n in range(NORMS)]
        std_ready = [sem(f"std_ready{n}") for n in range(NORMS)]
        shift_ready = [sem(f"shift_ready{n}") for n in range(NORMS)]
        h_ready = [sem(f"h_ready{n}") for n in range(NORMS)]
        t_ready, t_out = sem("t_ready"), sem("t_out")
        cnt_ready, cnt_kept, cnt_t_ready, adj_ready = sem("cnt_ready"), sem("cnt_kept"), sem("cnt_t_ready"), sem("adj_ready")
        inv_row_ready, deg_ready, deg_root_ready, wgt_deg_ready, wgt_deg_out = (
            sem("inv_row_ready"), sem("deg_ready"), sem("deg_root_ready"), sem("wgt_deg_ready"), sem("wgt_deg_out"))
        inv_root_ready, inv_cnt_ready = sem("inv_root_ready"), sem("inv_cnt_ready")
        hi_ready, lo_ready, acc_ready, hop_ready = sem("hi_ready"), sem("lo_ready"), sem("acc_ready"), sem("hop_ready")
        self_ready, self_out, msg_ready, msg_out, agg_ready, agg_out = (
            sem("self_ready"), sem("self_out"), sem("msg_ready"), sem("msg_out"), sem("agg_ready"), sem("agg_out"))
        up_ready, up_out, down_ready, down_out = sem("up_ready"), sem("up_out"), sem("down_ready"), sem("down_out")
        sup_ready, sup_out, sup_hi, gcn_ready, gcn_out = (
            sem("sup_ready"), sem("sup_out"), sem("sup_hi"), sem("gcn_ready"), sem("gcn_out"))
        mean_ready, mean_out = [sem(f"mean_ready{i}") for i in range(2)], [sem(f"mean_out{i}") for i in range(2)]
        sage_ready, sage_out = [sem(f"sage_ready{i}") for i in range(2)], [sem(f"sage_out{i}") for i in range(2)]
        relu_ready = sem("relu_ready")
        split_hi, split_ready = [sem(f"split_hi{i}") for i in range(2)], [sem(f"split_ready{i}") for i in range(2)]
        chain_sem = sem("run_chain")

        main, t_bank, cnt_bank, misc_bank = psum[0:4], psum[4:6], psum[6], psum[7]
        hop_bank = [None, psum[4:8], psum[0:4], psum[4:8]]
        in_bank, deg_bank = psum[7], psum[3]
        sage_bank = [psum[6], psum[7], psum[2], psum[3]]

        def row(ap):
            return ap.partition_broadcast(P)

        def tiled(ap, p=P):
            return ap.rearrange("(k p) n -> p k n", p=p)

        block = ctx.enter_context(nc.Block())

        @block.sync
        def _(sp):
            sp.dma_start(dw[:], row(dw_in)).then_inc(dw_loaded, 16)
            sp.dma_start(wself, tiled(wself_in)).then_inc(wself_loaded, 16)
            for to, of in ((bself, bself_in), (g1, g1_in), (be1, be1_in), (g2, g2_in), (be2, be2_in), (bf2, bf2_in)):
                sp.dma_start(to, row(of)).then_inc(rows_loaded, 16)
            for r in range(R):
                sp.dma_start(brel[r], row(brel_in[r])).then_inc(rel_rows_loaded, 16)
            sp.dma_start(bf1[:], bf1_in.rearrange("(g p) -> p g", p=P), allow_slow_non_contiguous=True)\
                .then_inc(bf1_loaded, 16)
            sp.wait_ge(lo_ready, NT)
            sp.wait_ge(acc_ready, NT)
            sp.dma_start(x[:], tiled(x_in)).then_inc(x_again_loaded, 16)
            for r in range(R):
                sp.dma_start(wrel[r], tiled(wrel_in[r])).then_inc(wrel_loaded[r], 16)
            sp.wait_ge(msg_ready, R * NT)
            sp.dma_start(wf1, tiled(wf1_in)).then_inc(wf1_loaded, 16)
            sp.dma_start(wf2, tiled(wf2_in)).then_inc(wf2_loaded, 16)
            sp.wait_ge(agg_ready, NT)
            sp.dma_start(sage_raw[0], tiled(wl1_in)).then_inc(sage_loaded[0], 16)
            sp.dma_start(w2, tiled(w2_in)).then_inc(w2_loaded, 16)
            sp.wait_ge(up_ready, GT)
            sp.dma_start(sage_raw[1], tiled(wr1_in)).then_inc(sage_loaded[1], 16)
            sp.dma_start(sage_raw[2], tiled(wl2_in)).then_inc(sage_loaded[2], 16)
            sp.wait_ge(down_ready, NT)
            sp.dma_start(sage_raw[3], tiled(wr2_in)).then_inc(sage_loaded[3], 16)
            for m in range(NT):
                sp.wait_ge(sage_out[1], m + 1)
                sp.dma_start(out[m * P:(m + 1) * P, :], x[:, m, :]).then_inc(out_stored, 16)
            sp.wait_ge(out_stored, 16 * NT)

        @block.gpsimd
        def _(pool):
            for t in range(NT):
                pool.wait_ge(hi_ready, t + 1)
                pool.tensor_tensor(lo[0][:, t, :], x[:, t, :], hi[0][:, t, :].bitcast(F32), ALU.subtract)\
                    .then_inc(lo_ready, 1)
            pool.tensor_tensor(wgt_sum, wall[:, 0, :, :], wall[:, 1, :, :], ALU.add).then_inc(wgt_add, 1)
            for r in range(2, R):
                pool.wait_ge(wgt_add, r - 1)
                pool.tensor_tensor(wgt_sum, wgt_sum, wall[:, r, :, :], ALU.add).then_inc(wgt_add, 1)
            pool.wait_ge(wgt_add, R - 1)
            pool.tensor_tensor(wgt_sum[:, 0:2, :], wgt_sum[:, 0:2, :], wgt_sum[:, 2:4, :], ALU.add).then_inc(wgt_add, 1)
            pool.wait_ge(wgt_add, R)
            pool.tensor_tensor(wgt_sum[:, 0, :], wgt_sum[:, 0, :], wgt_sum[:, 1, :], ALU.add).then_inc(wgt_add, 1)
            pool.tensor_copy(cnt_r[:], wall[:, R, :, :]).then_inc(cnt_r_ready, 1)
            pool.wait_ge(rows_loaded, 16 * 6)
            for t in range(NT):
                pool.wait_ge(t_ready, use_of(H_REL, t) + 1)
                pool.tensor_tensor(h[:, t, :], h[:, t, :], bself, ALU.add).then_inc(self_biased, 1)
                pool.wait_ge(h_ready[TO_REL], t + 1)
                pool.tensor_tensor(x[:, t, :], x[:, t, :], be2, ALU.add).then_inc(ln2_biased, 1)
            pool.wait_ge(msg_out, R * NT)
            for to, of in ((b2, b2_in), (bl1, bl1_in), (bl2, bl2_in)):
                pool.dma_start(to, row(of)).then_inc(late_rows_loaded, 16)
            for t in range(NT):
                pool.wait_ge(t_ready, use_of(H_FFN, t) + 1)
                pool.tensor_tensor(h[:, t, :], h[:, t, :], bf2, ALU.add).then_inc(ffn_biased, 1)
            pool.wait_ge(late_rows_loaded, 16 * 3)
            for t in range(NT):
                pool.wait_ge(h_ready[TO_GCN], t + 1)
                pool.tensor_tensor(x[:, t, :], x[:, t, :], b2, ALU.add).then_inc(gcn_biased, 1)
            for t in range(NT):
                pool.wait_ge(h_ready[TO_SAGE], t + 1)
                pool.wait_ge(split_hi[0], t + 1)
                pool.tensor_tensor(lo[1][:, t, :], h[:, t, :], hi[1][:, t, :].bitcast(F32), ALU.subtract)\
                    .then_inc(split_ready[0], 1)
            for t in range(NT):
                pool.tensor_tensor(x[:, t, :], x[:, t, :], bl2, ALU.add).then_inc(sage_biased, 1)

        @block.scalar
        def _(act):
            def root(n, t):
                act.wait_ge(var_ready[n], t + 1)
                act.activation(std[:, t:t + 1], mean_var[:, t, 1:2], ACT.Sqrt, bias=eps[:]).then_inc(std_ready[n], 1)

            def norm_relu(n, t):
                act.wait_ge(shift_ready[n], t + 1)
                act.activation(h[:, t, :], x[:, t, :], ACT.Relu, bias=shift[:, t:t + 1], scale=rstd[:, t:t + 1])\
                    .then_inc(h_ready[n], 1)

            def empty(use, to):
                act.wait_ge(t_ready, use + 1)
                act.activation(to, t_bank[use % 2][:].rearrange("p (a n) -> p a n", n=to.shape[-1]) if len(to.shape) == 3
                               else t_bank[use % 2][:], ACT.Copy).then_inc(t_out, 1)

            def empty_h(what, t):
                empty(use_of(what, t), h_t[:, :, t * P:(t + 1) * P])

            def empty_sage(what, q, k):
                empty(use_of(what, k), sage(q, k))

            for m in range(NT):
                act.activation(hi[0][:, m, :], x[:, m, :], ACT.Copy).then_inc(hi_ready, 1)
            act.wait_ge(inv_row_ready, 1)
            for i in range(1, HOPS):
                for m in range(NT):
                    act.wait_ge(hop_ready, (i - 1) * NT + m + 1)
                    act.activation(hi[i % 2][:, m, :], hop_bank[i][m][:], ACT.Copy, scale=inv_row[:, m:m + 1])\
                        .then_inc(hi_ready, 1)
            for t in range(NT):
                root(TO_REL, t)
                norm_relu(TO_REL, t)
                empty_h(H_REL, t)
            act.wait_ge(deg_ready, 1)
            act.activation(deg_root[:], out_deg[:], ACT.Sqrt).then_inc(deg_root_ready, 1)
            root(MID, 0)
            root(MID, 1)
            empty_h(H_FFN, 0)
            root(MID, 2)
            empty_h(H_FFN, 1)
            empty_h(H_FFN, 2)
            root(MID, 3)
            empty_h(H_FFN, 3)
            act.wait_ge(bf1_loaded, 16)
            for g in range(GT):
                act.wait_ge(up_ready, g + 1)
                act.activation(hid[:, g, :], main[g % 4][:], ACT.Gelu, bias=bf1[:, g:g + 1]).then_inc(up_out, 1)
                if g >= 4:
                    empty_sage(WL1, 0, g - 4)
            for t in range(NT):
                root(OUT_FFN, t)
                root(TO_GCN, t)
                norm_relu(TO_GCN, t)
                if t < 2:
                    empty_sage(WR1, 1, 2 * t)
                    empty_sage(WR1, 1, 2 * t + 1)
                elif t == 2:
                    empty_sage(WL2, 2, 0)
                    empty_h(H_GCN, 0)
                    empty_h(H_GCN, 1)
            empty_h(H_GCN, 2)
            for m in range(NT):
                act.wait_ge(sup_ready, m + 1)
                act.activation(hi[0][:, m, :], main[m][:], ACT.Copy, scale=inv_root[:, m:m + 1]).then_inc(sup_hi, 1)
                if m == 0:
                    empty_h(H_GCN, 3)
            for k in range(1, KT):
                empty_sage(WL2, 2, k)
            for t in range(NT):
                root(TO_SAGE, t)
                if 1 <= t < 3:
                    empty_h(H_SAGE1, t - 1)
                norm_relu(TO_SAGE, t)
                act.activation(hi[1][:, t, :], x[:, t, :], ACT.Relu, bias=shift[:, t:t + 1], scale=rstd[:, t:t + 1])\
                    .then_inc(split_hi[0], 1)
            for t in range(2, NT):
                empty_h(H_SAGE1, t)
            for k in range(KT):
                empty_sage(WR2, 3, k)
            for t in range(NT):
                act.wait_ge(sage_out[0], t + 1)
                act.activation(hi[0][:, t, :], h[:, t, :], ACT.Relu).then_inc(split_hi[1], 1)
                act.activation(h[:, t, :], h[:, t, :], ACT.Relu).then_inc(relu_ready, 1)
                if t > 0:
                    empty_h(H_SAGE2, t - 1)
            empty_h(H_SAGE2, NT - 1)

        @block.vector
        def _(dve):
            links = [0]

            def link(ins):
                links[0] += 1
                ins.then_inc(chain_sem, 1)
                dve.wait_ge(chain_sem, links[0])

            def moments(n, t, rows):
                link(dve.bn_stats(stats[:, t, :], rows))
                dve.bn_aggr(mean_var[:, t, :], stats[:, t, :]).then_inc(var_ready[n], 1)

            def inverse_std(n, t):
                dve.wait_ge(std_ready[n], t + 1)
                link(dve.reciprocal(rstd[:, t:t + 1], std[:, t:t + 1]))

            def scale_and_shift(n, t):
                inverse_std(n, t)
                dve.tensor_scalar(shift[:, t:t + 1], mean_var[:, t, 0:1], rstd[:, t:t + 1], -1.0, ALU.mult, ALU.mult)\
                    .then_inc(shift_ready[n], 1)

            def affine_norm(n, t, rows, gain, plus, to):
                inverse_std(n, t)
                link(dve.scalar_tensor_tensor(rows, rows, mean_var[:, t, 0:1], gain, ALU.subtract, ALU.mult))
                return dve.scalar_tensor_tensor(to, rows, rstd[:, t:t + 1], plus, ALU.mult, ALU.add)

            def eye_of(t):
                return eye[:, N - P - t * P:2 * N - P - t * P]

            for t in range(NT):
                link(dve.tensor_tensor(both_ways[:, t % 2, :], psum[t][:], count[t], ALU.add))
                dve.scalar_tensor_tensor(adj[:, t, :], both_ways[:, t % 2, :], 0.0, eye_of(t), ALU.is_gt, ALU.add,
                                         accum_out=row_sum[:, t:t + 1]).then_inc(adj_ready, 1)
            dve.wait_ge(adj_ready, NT)
            link(dve.tensor_scalar(inv_row[:], row_sum[:], 1.0, None, ALU.max))
            dve.reciprocal(inv_row[:], inv_row[:]).then_inc(inv_row_ready, 1)
            dve.wait_ge(cnt_ready, 1)
            dve.tensor_scalar(inv_cnt[:], in_bank[:], 1.0, None, ALU.max).then_inc(cnt_kept, 1)
            dve.wait_ge(dw_loaded, 16)
            dve.wait_ge(inv_row_ready, 1)
            for i in range(HOPS):
                link(dve.tensor_scalar(dw_inv[:, i, :], inv_row[:], dw[:, i + 1:i + 2], None, ALU.mult))
            for m in range(NT):
                dve.tensor_scalar(h[:, m, :], x[:, m, :], dw[:, 0:1], None, ALU.mult).then_inc(acc_ready, 1)
            for i in range(1, HOPS + 1):
                for m in range(NT):
                    rows = hop_bank[i][m]
                    if i < HOPS:
                        dve.wait_ge(hi_ready, i * NT + m + 1)
                        dve.scalar_tensor_tensor(lo[i % 2][:, m, :], rows[:], inv_row[:, m:m + 1],
                                                 hi[i % 2][:, m, :].bitcast(F32), ALU.mult, ALU.subtract).then_inc(lo_ready, 1)
                    else:
                        dve.wait_ge(hop_ready, (i - 1) * NT + m + 1)
                    dve.wait_ge(acc_ready, (i - 1) * NT + m + 1)
                    dve.scalar_tensor_tensor(h[:, m, :], rows[:], dw_inv[:, i - 1, m:m + 1], h[:, m, :], ALU.mult, ALU.add)\
                        .then_inc(acc_ready, 1)
                    if i == HOPS:
                        dve.wait_ge(acc_ready, i * NT + m + 1)
                        dve.wait_ge(x_again_loaded, 16)
                        link(dve.scalar_tensor_tensor(x[:, m, :], h[:, m, :], 0.0, x[:, m, :], ALU.max, ALU.add))
                        moments(TO_REL, m, x[:, m, :])
                        scale_and_shift(TO_REL, m)
            dve.wait_ge(wgt_deg_ready, 1)
            link(dve.tensor_scalar(wgt_deg[:], deg_bank[:, 0:NT], 1.0, None, ALU.max))
            dve.reciprocal(inv_wgt[:], wgt_deg[:]).then_inc(wgt_deg_out, 1)
            for m in range(NT):
                dve.wait_ge(self_ready, m + 1)
                dve.wait_ge(self_biased, m + 1)
                dve.tensor_tensor(h[:, m, :], main[m][:], h[:, m, :], ALU.add).then_inc(self_out, 1)
            for t in range(NT):
                link(dve.tensor_scalar(both_ways[:, t % 2, :], count[t], 0.0, None, ALU.is_gt))
                link(dve.tensor_reduce(out_deg[:, t:t + 1], both_ways[:, t % 2, :], AX.X, ALU.add))
            dve.tensor_scalar(out_deg[:], out_deg[:], 1.0, None, ALU.add).then_inc(deg_ready, 1)
            dve.wait_ge(rel_rows_loaded, 16 * R)
            for r in range(R):
                for m in range(NT):
                    dve.wait_ge(msg_ready, r * NT + m + 1)
                    dve.tensor_tensor(msg[r][:, m, :], main[m][:], brel[r], ALU.add).then_inc(msg_out, 1)
            dve.wait_ge(cnt_kept, 1)
            dve.reciprocal(inv_cnt[:], inv_cnt[:]).then_inc(inv_cnt_ready, 1)
            dve.wait_ge(deg_root_ready, 1)
            dve.reciprocal(inv_root[:], deg_root[:]).then_inc(inv_root_ready, 1)
            dve.wait_ge(wgt_deg_out, 1)
            for m in range(NT):
                dve.wait_ge(agg_ready, m + 1)
                dve.wait_ge(self_out, m + 1)
                dve.scalar_tensor_tensor(h[:, m, :], main[m][:], inv_wgt[:, m:m + 1], h[:, m, :], ALU.mult, ALU.add)\
                    .then_inc(agg_out, 1)
                dve.wait_ge(agg_out, m + 1)
                moments(MID, m, h[:, m, :])
                affine_norm(MID, m, h[:, m, :], g1, be1, h[:, m, :]).then_inc(h_ready[MID], 1)
            for m in range(NT):
                dve.wait_ge(down_ready, m + 1)
                dve.wait_ge(ffn_biased, m + 1)
                dve.tensor_tensor(h[:, m, :], main[m][:], h[:, m, :], ALU.add).then_inc(down_out, 1)
                dve.wait_ge(down_out, m + 1)
                moments(OUT_FFN, m, h[:, m, :])
                dve.wait_ge(ln2_biased, m + 1)
                link(affine_norm(OUT_FFN, m, h[:, m, :], g2, x[:, m, :], x[:, m, :]))
                moments(TO_GCN, m, x[:, m, :])
                scale_and_shift(TO_GCN, m)

            def gcn_adjacency(t):
                dve.wait_ge(cnt_t_ready, t + 1)
                half = misc_bank if t % 2 else cnt_bank
                dve.scalar_tensor_tensor(adj[:, t, :], half[:], 0.0, eye_of(t), ALU.is_gt, ALU.add).then_inc(adj_ready, 1)

            dve.wait_ge(inv_root_ready, 1)
            for half in range(2):
                pair = (2 * half, 2 * half + 1)
                for t in pair:
                    gcn_adjacency(t)
                for m in pair:
                    dve.wait_ge(sup_hi, m + 1)
                    dve.scalar_tensor_tensor(lo[0][:, m, :], main[m][:], inv_root[:, m:m + 1], hi[0][:, m, :].bitcast(F32),
                                             ALU.mult, ALU.subtract).then_inc(sup_out, 1)

            def split_rows(t):
                dve.wait_ge(relu_ready, t + 1)
                dve.wait_ge(split_hi[1], t + 1)
                dve.tensor_tensor(lo[0][:, t, :], h[:, t, :], hi[0][:, t, :].bitcast(F32), ALU.subtract)\
                    .then_inc(split_ready[1], 1)

            for m in range(NT):
                dve.wait_ge(gcn_ready, m + 1)
                dve.wait_ge(gcn_biased, m + 1)
                dve.scalar_tensor_tensor(x[:, m, :], main[m][:], inv_root[:, m:m + 1], x[:, m, :], ALU.mult, ALU.add)\
                    .then_inc(gcn_out, 1)
                dve.wait_ge(gcn_out, m + 1)
                moments(TO_SAGE, m, x[:, m, :])
                scale_and_shift(TO_SAGE, m)
            dve.wait_ge(inv_cnt_ready, 1)
            for layer in range(2):
                for k in range(KT):
                    dve.wait_ge(mean_ready[layer], k + 1)
                    dve.tensor_tensor(agg_t[layer][:, k, :], main[k][:], inv_cnt[:], ALU.mult).then_inc(mean_out[layer], 1)
                for m in range(NT):
                    dve.wait_ge(sage_ready[layer], m + 1)
                    if layer == 0:
                        dve.wait_ge(late_rows_loaded, 16 * 3)
                        dve.tensor_tensor(h[:, m, :], sage_bank[m][:], bl1, ALU.add).then_inc(sage_out[0], 1)
                        if m > 0:
                            split_rows(m - 1)
                    else:
                        dve.wait_ge(sage_biased, m + 1)
                        dve.tensor_tensor(x[:, m, :], sage_bank[m][:], x[:, m, :], ALU.add).then_inc(sage_out[1], 1)
                if layer == 0:
                    split_rows(NT - 1)

        @block.tensor
        def _(pe):
            slow = load_flag(pe, PE)

            def fill(use, blocks):
                if use >= 2:
                    pe.wait_ge(t_out, use - 1)
                for i, b in enumerate(blocks):
                    ins = pe.transpose(t_bank[use % 2][:, i * P:(i + 1) * P], b, ident[:])
                ins.then_inc(t_ready, 1)

            def fill_h(what, t, ready):
                pe.wait_ge(ready, t + 1)
                fill(use_of(what, t), [h[:, t, k * P:(k + 1) * P] for k in range(KT)])

            def fill_sage(what, q, k):
                pe.wait_ge(sage_loaded[q], 16)
                fill(use_of(what, k), [sage_raw[q][:, o, k * P:(k + 1) * P] for o in range(KT)])

            def transposed(what, t):
                pe.wait_ge(t_out, use_of(what, t) + 1)

            def product(bank, pairs, start=True, stop=True):
                for i, (left, right) in enumerate(pairs):
                    ins = pe.matmul(bank, left, right, start=start and i == 0, stop=stop and i == len(pairs) - 1)
                return ins

            def tile(t):
                return slice(t * P, (t + 1) * P)

            def rows_by(weight, m):
                return [(h_t[:, k, tile(m)], weight[:, k, :]) for k in range(KT)]

            def transpose_counts(tiles):
                for t in tiles:
                    if t >= 2:
                        pe.wait_ge(adj_ready, NT + t - 1)
                    bank = misc_bank if t % 2 else cnt_bank
                    for s in range(NT):
                        ins = pe.transpose(bank[:, tile(s)], count[s][:, tile(t)], ident[:])
                    ins.then_inc(cnt_t_ready, 1)

            product(in_bank[:], [(ones[:], count[s]) for s in range(NT)]).then_inc(cnt_ready, 1)
            for i in range(1, HOPS + 1):
                src = (i - 1) % 2

                def hop(m, s):
                    ins = product(hop_bank[i][m][:], [(adj[:, s, tile(m)], part[src][:, s, :]) for part in (hi, lo)],
                                  start=(s == 0), stop=(s == NT - 1))
                    if s == NT - 1:
                        ins.then_inc(hop_ready, 1)

                if i == HOPS:
                    pe.wait_ge(acc_ready, (i - 1) * NT)
                for s in range(NT):
                    if i == 1:
                        pe.wait_ge(adj_ready, s + 1)
                    pe.wait_ge(lo_ready, (i - 1) * NT + s + 1)
                    for m in range(2):
                        hop(m, s)
                if i == 1:
                    pe.wait_ge(cnt_kept, 1)
                for m in range(2, NT):
                    for s in range(NT):
                        hop(m, s)
            fill_h(H_REL, 0, h_ready[TO_REL])
            pe.wait_ge(wgt_add, R + 1)
            pe.wait_ge(acc_ready, HOPS * NT)
            for m in range(NT):
                ins = product(deg_bank[:, m:m + 1], [(wgt_sum[:, 0, tile(m)], ones[:, 0:1])])
            ins.then_inc(wgt_deg_ready, 1)
            pe.wait_ge(wself_loaded, 16)
            for m in range(NT):
                transposed(H_REL, m)
                if m == NT - 1:
                    pe.wait_ge(wgt_deg_out, 1)
                pairs = rows_by(wself, m)
                product(main[m][:], pairs[:KT // 2], stop=False)
                if m + 1 < NT:
                    fill_h(H_REL, m + 1, h_ready[TO_REL])
                product(main[m][:], pairs[KT // 2:], start=False).then_inc(self_ready, 1)
            for r in range(R):
                pe.wait_ge(wrel_loaded[r], 16)
                for m in range(NT):
                    if r == 0:
                        pe.wait_ge(self_out, m + 1)
                    else:
                        pe.wait_ge(msg_out, (r - 1) * NT + m + 1)
                    product(main[m][:], rows_by(wrel[r], m)).then_inc(msg_ready, 1)
            for m in range(NT):
                for r in range(R):
                    for s in range(NT):
                        if m == 0:
                            pe.wait_ge(msg_out, max(r * NT + s, (R - 1) * NT) + 1)
                        if m > 0 and r == R // 2 and s == 0:
                            fill_h(H_FFN, m - 1, h_ready[MID])
                        ins = pe.matmul(main[m][:], wall[:, r, s, tile(m)], msg[r][:, s, :],
                                        start=(r == 0 and s == 0), stop=(r == R - 1 and s == NT - 1))
                ins.then_inc(agg_ready, 1)
            pe.wait_ge(wf1_loaded, 16)

            def up(g, nodes):
                return product(main[g % 4][:, nodes], [(wf1[:, k, tile(g)], h_t[:, k, nodes]) for k in range(KT)])

            transposed(H_FFN, NT - 2)
            for g in range(4):
                pe.wait_ge(agg_out, g + 1)
                up(g, slice(0, N - P))
                if g == 1:
                    fill_h(H_FFN, NT - 1, h_ready[MID])
            transposed(H_FFN, NT - 1)
            for g in range(4):
                up(g, slice(N - P, N)).then_inc(up_ready, 1)
            for g in range(4, GT):
                pe.wait_ge(up_out, g - 3)
                up(g, slice(0, N)).then_inc(up_ready, 1)
                fill_sage(WL1, 0, g - 4)
            pe.wait_ge(wf2_loaded, 16)
            late_fills = {(1, 6): (WR1, 0), (1, 7): (WR1, 1), (2, 6): (WR1, 2), (2, 7): (WR1, 3), (3, 6): (WL2, 0)}
            for m in range(NT):
                for g in range(GT):
                    if m == 0:
                        pe.wait_ge(up_out, max(g + 1, 5))
                    elif g == 0 and m + 5 <= GT:
                        pe.wait_ge(up_out, m + 5)
                    if (m, g) in late_fills:
                        what, k = late_fills[m, g]
                        fill_sage(what, 1 if what == WR1 else 2, k)
                    elif (m, g) == (3, 7):
                        fill_h(H_GCN, 0, h_ready[TO_GCN])
                    ins = pe.matmul(main[m][:], hid[:, g, tile(m)], wf2[:, g, :], start=(g == 0), stop=(g == GT - 1))
                ins.then_inc(down_ready, 1)
            fill_h(H_GCN, 1, h_ready[TO_GCN])
            transpose_counts(range(2))
            pe.wait_ge(w2_loaded, 16)
            for m in range(NT):
                transposed(H_GCN, m)
                pe.wait_ge(down_out, m + 1)
                product(main[m][:], rows_by(w2, m)).then_inc(sup_ready, 1)
                if m < 2:
                    fill_h(H_GCN, m + 2, h_ready[TO_GCN])
                if m == 1:
                    transpose_counts(range(2, NT))
            fill_sage(WL2, 2, 1)
            fill_sage(WL2, 2, 2)

            def gcn(m, s):
                ins = product(main[m][:], [(adj[:, s, tile(m)], part[0][:, s, :]) for part in (hi, lo)],
                              start=(s == 0), stop=(s == NT - 1))
                if s == NT - 1:
                    ins.then_inc(gcn_ready, 1)

            pe.wait_ge(adj_ready, 2 * NT)
            for s in range(NT):
                pe.wait_ge(sup_out, s + 1)
                if s < 2:
                    pe.wait_ge(sup_out, 2)
                for m in range(2):
                    gcn(m, s)
            fill_sage(WL2, 2, 3)
            for m in range(2, NT):
                for s in range(NT):
                    if (m, s) == (NT - 1, NT - 1):
                        fill_h(H_SAGE1, 0, h_ready[TO_SAGE])
                    gcn(m, s)

            def means(layer, exact):
                for k in range(KT):
                    if exact:
                        pairs = [(part[1 - layer][:, s, tile(k)], cnt_r[:, s, :]) for s in range(NT) for part in (hi, lo)]
                    else:
                        pairs = [(h[:, s, tile(k)], count[s]) for s in range(NT)]
                    product(main[k][:], pairs).then_inc(mean_ready[layer], 1)
                    if layer == 0:
                        fill_sage(WR2, 3, k)

            for layer in range(2):
                what, ready = ((H_SAGE1, h_ready[TO_SAGE]), (H_SAGE2, relu_ready))[layer]
                wl, wr = 2 * layer, 2 * layer + 1

                def own(m, then=None):
                    transposed(what, m)
                    pairs = [(h_t[:, k, tile(m)], sage(wr, k)) for k in range(KT)]
                    product(sage_bank[m][:], pairs[:KT // 2], stop=False)
                    if then:
                        fill_h(what, then, ready)
                    product(sage_bank[m][:], pairs[KT // 2:], start=False, stop=False)

                if layer == 0:
                    pe.wait_ge(adj_ready, 2 * NT)
                    own(0, 1)
                    own(1, 2)
                    fill_h(what, 3, ready)
                else:
                    pe.wait_ge(sage_out[0], 2)
                    for m in range(2):
                        own(m)
                        fill_h(what, m + 2, ready)
                pe.wait_ge(split_ready[layer], NT)
                if layer == 0:
                    pe.wait_ge(gcn_out, NT)
                    pe.wait_ge(cnt_r_ready, 1)
                else:
                    pe.wait_ge(sage_out[0], NT)
                with pe.If_eq(slow, 0):
                    means(layer, True)
                with pe.If_ne(slow, 0):
                    means(layer, False)
                for m in range(NT):
                    if m >= 2:
                        pe.wait_ge(mean_out[layer], m + 1)
                        own(m)
                    for k in range(KT):
                        if m == 0:
                            pe.wait_ge(mean_out[layer], k + 1)
                        ins = pe.matmul(sage_bank[m][:], agg_t[layer][:, k, tile(m)], sage(wl, k),
                                        start=False, stop=(k == KT - 1))
                    ins.then_inc(sage_ready[layer], 1)
                    if layer == 0 and 1 <= m < 3:
                        fill_h(H_SAGE2, m - 1, relu_ready)


_INS = ['x', 'src', 'dst', 'edge_type_4', 'edge_weight', 'L0_gnn_W', 'L0_gnn_b', 'L0_gnn_diffusion_weights',
        'L1_gnn_W_self', 'L1_gnn_b_self', 'L1_gnn_W_rel', 'L1_gnn_b_rel', 'L1_gnn_ln1_g', 'L1_gnn_ln1_b', 'L1_gnn_ln2_g',
        'L1_gnn_ln2_b', 'L1_gnn_W_ffn1', 'L1_gnn_b_ffn1', 'L1_gnn_W_ffn2', 'L1_gnn_b_ffn2', 'L2_gnn_weight', 'L2_gnn_bias',
        'L3_gnn_Wl1', 'L3_gnn_bl1', 'L3_gnn_Wr1', 'L3_gnn_Wl2', 'L3_gnn_bl2', 'L3_gnn_Wr2']


def kernel(**inputs):
    import numpy as _np
    import concourse.bacc as _bacc
    from concourse import mybir as _mybir
    from concourse.bass_utils import run_bass_kernel_spmd as _run

    nc = _bacc.Bacc("TRN2", target_bir_lowering=False, num_devices=1)
    arrays, args = {}, []
    for name in _INS:
        a = _np.ascontiguousarray(inputs[name])
        arrays[f"in_{name}"] = a
        args.append(nc.dram_tensor(f"in_{name}", a.shape, _mybir.dt.from_np(a.dtype), kind="ExternalInput").ap())
    args.append(nc.dram_tensor("out", (N, D), F32, kind="ExternalOutput").ap())
    gnn_program(nc, *args)
    r = _run(nc, [arrays], core_ids=[0])
    return r.results[0]["out"]
```
